# Optimizing a Trainium2 kernel written in Bass

```python
import numpy as np
import jax
import jax.numpy as jnp

def _softmax(x, axis=-1):
    return jax.nn.softmax(x, axis=axis)

def _gelu(x):
    return jax.nn.gelu(x, approximate=True)

def _silu(x):
    return jax.nn.silu(x)

def _sigmoid(x):
    return jax.nn.sigmoid(x)

def _layernorm(x, axis=-1, eps=1e-05):
    m = jnp.mean(x, axis=axis, keepdims=True)
    v = jnp.var(x, axis=axis, keepdims=True)
    return (x - m) / jnp.sqrt(v + eps)

def _scatter_add(tgt, idx, src, axis=0):
    return tgt.at[idx].add(src)

def _segment_sum(src, seg, n):
    return jax.ops.segment_sum(src, seg, n)
kernel_name = 'mk_conv_attn_hybrid_d2_conv_nchw128_r2_78ef41'

def setup_inputs(seed: int=0):
    np.random.seed(seed)
    _w = jnp.asarray

    def _rec_inputs():
        import jax
        import jax.numpy as jnp
        _gk = jax.random.key(seed)
        x = -0.0005207 + 1.001 * jax.random.normal(jax.random.fold_in(_gk, 1), (4, 64, 32, 32), jnp.float32)
        return x
    x = _rec_inputs()

    def _L0_conv_setup():
        import jax, jax.numpy as jnp
        import numpy as np
        B, C, H, W = (4, 64, 32, 32)
        MEDIA_C = 32
        key = jax.random.key(seed)
        ks = jax.random.split(key, 5)
        return {'x': jax.random.normal(ks[0], (B, C, H, W), dtype=jnp.float32), 'wq': jax.random.normal(ks[1], (MEDIA_C, C), dtype=jnp.float32) * (1.0 / np.sqrt(C)), 'wk': jax.random.normal(ks[2], (MEDIA_C, C), dtype=jnp.float32) * (1.0 / np.sqrt(C)), 'wv': jax.random.normal(ks[3], (MEDIA_C, C), dtype=jnp.float32) * (1.0 / np.sqrt(C)), 'wo': jax.random.normal(ks[4], (C, MEDIA_C), dtype=jnp.float32) * (1.0 / np.sqrt(MEDIA_C))}
    _L0_conv_all = _L0_conv_setup()
    _L0_conv_in = {k: v for k, v in _L0_conv_all.items() if k in ('wq', 'wk', 'wv', 'wo')}
    del _L0_conv_all

    def _L1_attn_setup():
        import jax, jax.numpy as jnp
        import numpy as np
        key = jax.random.key(seed)
        inputs = jax.random.normal(key, (4, 2048, 64), dtype=jnp.float32)
        return {'inputs': inputs}
    _L1_attn_all = _L1_attn_setup()
    _L1_attn_in = {k: v for k, v in _L1_attn_all.items() if k in ()}
    del _L1_attn_all

    def _L1_ffn_setup():
        import jax, jax.numpy as jnp
        import numpy as np
        B, N, D, C, E, K = (8, 4096, 64, 64, 8, 2)
        key = jax.random.key(seed)
        k0, k1, k2 = jax.random.split(key, 3)
        x = jax.random.normal(k0, (B, N, D), dtype=jnp.float32)
        router_w = jax.random.normal(k1, (D, E), dtype=jnp.float32) * 0.05
        router_b = jnp.zeros((E,), dtype=jnp.float32)
        expert_w = jax.random.normal(k2, (E, D, C), dtype=jnp.float32) * (1.0 / np.sqrt(D))
        expert_b = jnp.zeros((E, C), dtype=jnp.float32)
        return {'x': x, 'router_w': router_w, 'router_b': router_b, 'expert_w': expert_w, 'expert_b': expert_b}
    _L1_ffn_all = _L1_ffn_setup()
    _L1_ffn_in = {k: v for k, v in _L1_ffn_all.items() if k in ('router_w', 'router_b', 'expert_w', 'expert_b')}
    del _L1_ffn_all
    return {'x': x, 'L0_conv_wq': _L0_conv_in['wq'], 'L0_conv_wk': _L0_conv_in['wk'], 'L0_conv_wv': _L0_conv_in['wv'], 'L0_conv_wo': _L0_conv_in['wo'], 'L1_ffn_router_w': _L1_ffn_in['router_w'], 'L1_ffn_router_b': _L1_ffn_in['router_b'], 'L1_ffn_expert_w': _L1_ffn_in['expert_w'], 'L1_ffn_expert_b': _L1_ffn_in['expert_b']}

def reference(x, L0_conv_wq, L0_conv_wk, L0_conv_wv, L0_conv_wo, L1_ffn_router_w, L1_ffn_router_b, L1_ffn_expert_w, L1_ffn_expert_b):
    import jax
    import jax.numpy as jnp

    def _L0_conv_ref(x, wq, wk, wv, wo):
        import jax, jax.numpy as jnp
        import numpy as np
        B, C, H, W = (4, 64, 32, 32)
        MEDIA_C = 32
        b, c, h, w = x.shape
        n = h * w
        xf = x.reshape(b, c, n)
        q = jnp.einsum('mc,bcn->bmn', wq, xf)
        k = jnp.einsum('mc,bcn->bmn', wk, xf)
        v = jnp.einsum('mc,bcn->bmn', wv, xf)
        att = jnp.einsum('bmi,bmj->bij', k, q)
        att = jax.nn.softmax(att, axis=2)
        agg = jnp.einsum('bij,bmj->bmi', att, v)
        out = x + jnp.einsum('cm,bmn->bcn', wo, agg).reshape(b, c, h, w)
        return out

    def _L1_attn_ref(inputs):
        import jax, jax.numpy as jnp
        import numpy as np
        scores = jnp.einsum('bqd,bkd->bqk', inputs, inputs)
        weights = jax.nn.softmax(scores, axis=-1)
        out = jnp.einsum('bqk,bkd->bqd', weights, inputs)
        return out

    def _L1_ffn_ref(x, router_w, router_b, expert_w, expert_b):
        import jax, jax.numpy as jnp
        import numpy as np
        B, N, D, C, E, K = (8, 4096, 64, 64, 8, 2)
        router_probs = jax.nn.softmax(x @ router_w + router_b, axis=-1)
        top_p, top_i = jax.lax.top_k(router_probs, K)
        top_p = top_p / jnp.sum(top_p, axis=-1, keepdims=True)
        expert_out = jnp.einsum('bnd,edc->bnec', x, expert_w) + expert_b
        gathered = jnp.take_along_axis(expert_out, top_i[..., None], axis=2)
        return jnp.einsum('bnk,bnkc->bnc', top_p, gathered)

    def _gn(v, G=32, eps=1e-05):
        B_, C_, H_, W_ = v.shape
        g = v.reshape(B_, G, C_ // G, H_, W_)
        m = jnp.mean(g, axis=(2, 3, 4), keepdims=True)
        s = jnp.var(g, axis=(2, 3, 4), keepdims=True)
        return ((g - m) / jnp.sqrt(s + eps)).reshape(v.shape)

    def _ln_c(v, eps=1e-06):
        m = jnp.mean(v, axis=1, keepdims=True)
        s = jnp.var(v, axis=1, keepdims=True)
        return (v - m) / jnp.sqrt(s + eps)

    def _ln_t(v, eps=1e-05):
        m = jnp.mean(v, axis=-1, keepdims=True)
        s = jnp.var(v, axis=-1, keepdims=True)
        return (v - m) / jnp.sqrt(s + eps)

    def _to_tokens(v):
        B_, C_, H_, W_ = v.shape
        return v.reshape(B_, C_, H_ * W_).transpose(0, 2, 1)

    def _from_tokens(t, like):
        B_, C_, H_, W_ = like.shape
        return t.transpose(0, 2, 1).reshape(B_, C_, H_, W_)
    x = _L0_conv_ref(x, L0_conv_wq, L0_conv_wk, L0_conv_wv, L0_conv_wo)
    t = _to_tokens(x)
    t = t + _L1_attn_ref(_ln_t(t))
    t = t + _L1_ffn_ref(_ln_t(t), L1_ffn_router_w, L1_ffn_router_b, L1_ffn_expert_w, L1_ffn_expert_b)
    x = _from_tokens(t, x)
    return x

_drawn_inputs = setup_inputs


def setup_inputs(seed=0):
    import zlib

    import numpy as np

    out = dict(_drawn_inputs(seed))
    spreads = {'L1_ffn_router_b': (0.0, 0.1), 'L1_ffn_expert_b': (0.0, 0.274)}
    factors = {}
    for name, (base, spread) in spreads.items():
        noise = np.random.default_rng([zlib.crc32(name.encode()), seed]).standard_normal(out[name].shape)
        drawn = base * np.exp(spread * noise) if base else spread * noise
        out[name] = jnp.asarray(drawn.astype(out[name].dtype))
    for name, factor in factors.items():
        out[name] = (out[name] * factor).astype(out[name].dtype)
    return out
```

```python
from contextlib import ExitStack

import concourse.bass as bass
from concourse import mybir

ALU = mybir.AluOpType
ACT = mybir.ActivationFunctionType
AX = mybir.AxisListType
F32 = mybir.dt.float32
F32R = mybir.dt.float32r
F16 = mybir.dt.float16

P = 128
B, C, N, M, E = 4, 64, 1024, 32, 8
CHUNK = 512
T = N // P
EPS = 1e-5
ONE = M
ROW = 3 * M
SHIFT = float(C) / 2
LOWEST = -3.0e38

RING = 3
MX_AT = [[0], [1], [2, 3], [4], [5], [6], [7], []]
FIRST = ["w3", "wo", "q", "k", "vx"] + [f"mx{i}" for i in range(T)] + ["mrow"] + [f"st{j}" for j in range(T)] + ["po"]
BODY = ["q", "k", "vx", "uT"]
LAST = ["uT"]
for j in range(T):
    BODY += [f"s{j}"] + [f"mx{i}" for i in MX_AT[j]] + ["yT-"] * (j == 3)
    LAST += [f"s{j}"] + ["yT-"] * (j == 3)
BODY += ["mrow"]
for j in range(T):
    BODY += [f"st{j}"] + {0: ["oT"], 3: ["wT"], 5: ["rt"], 6: ["e0"], 7: ["e1"]}.get(j, [])
BODY += ["e2", "po", "gT", "e3"]
LAST += ["oT", "wT", "rt", "e0", "gT", "e1", "e2", "e3", "yT"]
assert len(BODY) % RING == 0


def col(tile):
    return (tile % 2) * CHUNK + (tile // 2) * P


def build(nc, x, wq, wk, wv, wo, rw, rb, ew, eb, out):
    ctx = ExitStack()
    with ctx:
        def sb(name, shape, dt=F32):
            return ctx.enter_context(nc.sbuf_tensor(name, shape, dt))

        def sem(name):
            return ctx.enter_context(nc.semaphore(name))

        ident = sb("ident", [P, P])
        ident_h = sb("ident_h", [P, P], F16)
        ident_r = sb("ident_r", [P, P], F32R)
        minus_half = sb("minus_half", [P, T])
        shift = sb("shift", [P, 1])
        ramp = sb("ramp", [P, T, E])
        w3 = sb("w3", [ROW, 2, C])
        wo4 = sb("wo4", [C, 4, M])
        w1 = sb("w1", [P, 2, 3, M], F32R)
        w2 = sb("w2", [P, 2, 3, M], F32R)
        vx1 = sb("vx1", [P, M + C], F32R)
        vx2 = sb("vx2", [P, M + C], F32R)
        wo_blk = sb("wo_blk", [P, 2, C + 1])
        e_in = sb("e_in", [P, E, C])
        e1 = sb("e1", [P, E * C], F32R)
        e2 = sb("e2", [P, E * C], F32R)
        r_in = sb("r_in", [P, E])
        r1 = sb("r1", [P, E], F32R)
        r2 = sb("r2", [P, E], F32R)
        rb_all = sb("rb_all", [P, E])
        eb_in = sb("eb_in", [T * E, C])
        eb_blk = sb("eb_blk", [T * E, T, C])
        tile_mask = sb("tile_mask", [T * E, T])

        xin = sb("xin", [P, B + 1, N])
        xst = sb("xst", [P, N], F32R)
        qst = sb("qst", [P, N], F32R)
        kst = sb("kst", [P, N], F32R)
        val = sb("val", [P, T, C])
        xt = sb("xt", [P, T, C])
        rowmax = sb("rowmax", [P, T])
        nmax = sb("nmax", [P, T, ROW + 2], F32R)
        nmax_f = sb("nmax_f", [P, T])
        prob1 = sb("prob1", [P, 2, N])
        prob2 = sb("prob2", [P, 2, N])
        agg = sb("agg", [P, CHUNK])
        rinv1 = sb("rinv1", [P, T])
        tok1 = sb("tok1", [P, T, C])
        tdiv = sb("tdiv", [P, T, C])
        stats1 = sb("stats1", [P, T, 6])
        sm1 = sb("sm1", [P, 6, T])
        u = sb("u", [P, T, C])
        uhl = sb("uhl", [P, T, 3, C], F16)
        zst = sb("zst", [P, N], F16)
        zsw = sb("zsw", [P, N], F16)
        rsum2 = sb("rsum2", [P, T])
        rinv2 = sb("rinv2", [P, T])
        att2 = sb("att2", [P, CHUNK])
        tok2 = sb("tok2", [P, T, C])
        odiv = sb("odiv", [P, T, C])
        stats2 = sb("stats2", [P, T, 6])
        sm2 = sb("sm2", [P, 6, T])
        wdup = sb("wdup", [P, T, 2, C])
        wst = sb("wst", [P, N], F32R)
        lg = sb("lg", [P, T, E])
        lg2 = sb("lg2", [P, T, E])
        cand = sb("cand", [P, T, E])
        pick1 = sb("pick1", [P, T, E])
        pick2 = sb("pick2", [P, T, E])
        gm = sb("gm", [P, 8, T])
        gate = sb("gate", [P, 2 * T, E])
        gate_t = sb("gate_t", [T * E, P])
        prod = sb("prod", [P, 2, 2, E, C])
        half = sb("half", [P, 2, E // 2, C])
        quart = sb("quart", [P, 2, E // 4, C])
        ysum = sb("ysum", [P, T, C])
        ybias = sb("ybias", [P, T, C])
        yres = sb("yres", [P, T, C])
        y = sb("y", [P, T, C])
        ob = sb("ob", [P, CHUNK])

        ring = ctx.enter_context(nc.psum_tensor("ring", [P, RING, 2, CHUNK], F32))
        acc1 = ctx.enter_context(nc.psum_tensor("acc1", [P, CHUNK], F32))
        acc2 = ctx.enter_context(nc.psum_tensor("acc2", [P, CHUNK], F32))

        s_fill = sem("ring_filled")
        s_const = sem("const_ready")
        s_pool = sem("pool_step")
        s_shift = sem("shift_ready")
        s_w3 = sem("w3_loaded")
        s_wol = sem("wo_loaded")
        s_ew = sem("experts_loaded")
        s_x = [sem(f"x_loaded{b}") for b in range(B)]
        s_wr1 = sem("weights_rounded")
        s_wts = sem("weights_split")
        s_wblk = sem("wo_blk_ready")
        s_er = sem("experts_rounded")
        s_es = sem("experts_split")
        s_xr = sem("x_rounded")
        s_xs = sem("x_split")
        s_qkr = sem("qk_rounded")
        s_qks = sem("qk_split")
        s_vx = sem("v_and_x_ready")
        s_mx = sem("rowmax_ready")
        s_nm = sem("negmax_split")
        s_mrow = sem("maxrow_ready")
        s_p1 = sem("probs1_ready")
        s_av1 = sem("agg_summed")
        s_agg = sem("agg_ready")
        s_po = sem("projection_read")
        s_t1 = sem("tok1_step")
        s_tk1 = sem("tok1_ready")
        s_ln1 = sem("ln1_step")
        s_ve1 = sem("var1_ready")
        s_rs1 = sem("rstd1_ready")
        s_un = sem("u_step")
        s_u = sem("uhl_ready")
        s_z = sem("z_ready")
        s_p2 = sem("probs2_ready")
        s_av2 = sem("att2_summed")
        s_att2 = sem("att2_ready")
        s_oT = sem("att2_read")
        s_t2 = sem("rinv2_ready")
        s_tk2 = sem("tok2_ready")
        s_ln2 = sem("ln2_step")
        s_ve2 = sem("var2_ready")
        s_rs2 = sem("rstd2_ready")
        s_w = sem("w_ready")
        s_wr = sem("w_rounded")
        s_ws = sem("w_split")
        s_lg = sem("logits_ready")
        s_top = sem("top2_step")
        s_gap = sem("logit_gap_ready")
        s_eg = sem("gap_exp_ready")
        s_gs = sem("gates_step")
        s_gate = sem("gates_ready")
        s_gt = sem("gates_transposed")
        s_gb = sem("expert_bias_summed")
        s_gbs = sem("ybias_ready")
        s_prod = sem("prods_ready")
        s_half = sem("prods_used")
        s_tree = sem("tree_step")
        s_y = sem("y_ready")
        s_ob = sem("out_ready")
        s_out = sem("out_stored")
        s_ob_free = sem("ob_free")

        RELEASE = {"w3": (s_wts, 3, 3), "wo": (s_wblk, 2, 2), "q": (s_qks, 2, 1), "k": (s_qks, 2, 2), "vx": (s_vx, 2, 2),
                   "mrow": (s_mrow, 1, 1), "po": (s_po, 1, 1), "uT": (s_z, 2, 2), "oT": (s_oT, 1, 1),
                   "wT": (s_ws, 1, 1), "rt": (s_lg, 1, 1), "gT": (s_gt, 1, 2), "yT": (s_ob, 1, 2), "yT-": (s_ob, 1, 2)}
        RELEASE.update({f"mx{i}": (s_mx, T, i + 1) for i in range(T)})
        RELEASE.update({f"st{j}": (s_p1, T, j + 1) for j in range(T)})
        RELEASE.update({f"s{j}": (s_p2, T, j + 1) for j in range(T)})
        RELEASE.update({f"e{g}": (s_prod, T // 2, T // 2 + g + 1) for g in range(T // 2)})
        NEXT = {"q", "k", "vx", "mrow", "po"} | {f"mx{i}" for i in range(T)} | {f"st{j}" for j in range(T)}

        def release(name, part, i):
            s, per, at = RELEASE[name]
            image = i + (part == "body" and name in NEXT) - (name == "yT-")
            return s, image * per + at

        def place(part, name, i):
            if part == "first":
                idx = FIRST.index(name)
                return idx % RING, idx, (FIRST[idx - RING], "first", 0) if idx >= RING else None
            if part == "body":
                idx = BODY.index(name)
                before = (BODY[idx - RING], "body", i if idx >= RING else i - 1)
                return (len(FIRST) + idx) % RING, len(FIRST) + i * len(BODY) + idx, before
            idx = LAST.index(name)
            before = (LAST[idx - RING], "last", B - 1) if idx >= RING else (BODY[idx - RING], "body", B - 2)
            return (len(FIRST) + idx) % RING, len(FIRST) + (B - 1) * len(BODY) + idx, before

        class Steps:

            def __init__(self, engine, s, per_image, b):
                self.engine, self.s, self.per, self.base, self.n = engine, s, per_image, b * per_image, 0

            def then(self, instruction):
                self.n += 1
                instruction.then_inc(self.s, 1)
                self.engine.wait_ge(self.s, self.base + self.n)

            def end(self):
                assert self.n == self.per, (self.n, self.per)

        block = ctx.enter_context(nc.Block())

        @block.sync
        def _(sp):
            for h in range(2):
                sp.dma_start(xin[h * C:(h + 1) * C, 0, :], x[0].rearrange("c h w -> c (h w)")).then_inc(s_x[0], 16)
                for n, w in enumerate((wq, wk, wv)):
                    sp.dma_start(w3[n * M:(n + 1) * M, h, :], w).then_inc(s_w3, 16)
            sp.wait_ge(s_const, 1)
            for h in range(2):
                sp.dma_start(wo4[:, 2 * h, :], wo).then_inc(s_wol, 16)
            for b in range(1, B):
                for h in range(2):
                    sp.dma_start(xin[h * C:(h + 1) * C, b, :], x[b].rearrange("c h w -> c (h w)")).then_inc(s_x[b], 16)
            for h in range(2):
                sp.dma_start(e_in[h * C:(h + 1) * C, :, :], ew.rearrange("e d c -> d e c")).then_inc(s_ew, 16)
                sp.dma_start(r_in[h * C:(h + 1) * C, :], rw).then_inc(s_ew, 16)
            sp.dma_start(rb_all[:, :], rb.rearrange("(a e) -> a e", a=1).to_broadcast([P, E])).then_inc(s_ew, 16)
            for t in range(T):
                sp.dma_start(eb_in[t * E:(t + 1) * E, :], eb).then_inc(s_ew, 16)

            def store(b, image):
                sp.wait_ge(s_ob, b + 2)
                for h in range(2):
                    sp.dma_start(image[:, h * CHUNK:(h + 1) * CHUNK], ob[h * C:(h + 1) * C, :]).then_inc(s_out, 16)
                sp.wait_ge(s_out, 2 * 16 * (b + 1))
                sp.sem_inc(s_ob_free, 1)

            flat = out.rearrange("b c h w -> (b c) (h w)")
            sp.sem_inc(s_ob_free, 2)
            with sp.Fori(0, B - 1) as i:
                store(i, flat[bass.ds(i * C, C), :])
            store(B - 1, flat[(B - 1) * C:B * C, :])

        @block.gpsimd
        def _(pool):
            pool.memset(wo4[:, :, :], 0.0).then_inc(s_const, 1)
            pool.memset(ident[:, :], 0.0).then_inc(s_pool, 1)
            pool.wait_ge(s_pool, 1)
            pool.affine_select(out=ident[:, :], in_=ident[:, :], compare_op=ALU.not_equal, fill=1.0, base=0,
                               pattern=[[-1, P]], channel_multiplier=1).then_inc(s_const, 1)
            pool.memset(nmax[:, :, :].bitcast(F32), 0.0)
            pool.memset(val[:, :, M + 1:C], 0.0)
            pool.memset(val[:, :, ONE:ONE + 1], 1.0).then_inc(s_const, 1)
            pool.memset(wo_blk[:, :, :], 0.0).then_inc(s_const, 1)
            pool.memset(minus_half[:, :], -0.5)
            pool.memset(y[:, :, :], 0.0).then_inc(s_y, 1)
            pool.memset(gate[:, T:2 * T, :], 0.0)
            pool.memset(xin[:, B, :], 0.0)
            for e in range(E):
                last = pool.memset(ramp[:, :, e:e + 1], float(E - e))
            pool.memset(tile_mask[:, :], 1.0).then_inc(s_pool, 1)
            pool.wait_ge(s_pool, 2)
            pool.affine_select(out=tile_mask[:, :], in_=tile_mask[:, :], compare_op=ALU.is_ge, fill=0.0, base=0,
                               pattern=[[-E, T]], channel_multiplier=1).then_inc(s_pool, 1)
            pool.wait_ge(s_pool, 3)
            pool.affine_select(out=tile_mask[:, :], in_=tile_mask[:, :], compare_op=ALU.is_ge, fill=0.0, base=E - 1,
                               pattern=[[E, T]], channel_multiplier=-1).then_inc(s_const, 1)

            def rstd(b, s_ve, s_rs, sm):
                pool.wait_ge(s_ve, b + 1)
                pool.tensor_tensor(sm[:, 3, :], sm[:, 2, :], minus_half[:, :], ALU.pow).then_inc(s_rs, 1)

            def sum_experts(b, more):
                tree = Steps(pool, s_tree, 2 * (T // 2) + 1, b)
                for g in range(T // 2):
                    if g == 3 and more:
                        rstd(b + 1, s_ve1, s_rs1, sm1)
                    pool.wait_ge(s_prod, (T // 2) * (b + 1) + g + 1)
                    p = prod[:, g % 2]
                    pool.tensor_tensor(half[:, :, :, :], p[:, :, 0:4, :], p[:, :, 4:8, :], ALU.add).then_inc(s_half, 1)
                    pool.wait_ge(s_half, (T // 2) * b + g + 1)
                    tree.then(pool.tensor_tensor(quart[:, :, :, :], half[:, :, 0:2, :], half[:, :, 2:4, :], ALU.add))
                    tree.then(pool.tensor_tensor(ysum[:, 2 * g:2 * g + 2, :], quart[:, :, 0, :], quart[:, :, 1, :], ALU.add))
                tree.then(pool.tensor_tensor(yres[:, :, :], ysum[:, :, :], tok2[:, :, :], ALU.add))
                tree.end()
                pool.wait_ge(s_gbs, b + 1)
                pool.tensor_tensor(y[:, :, :], yres[:, :, :], ybias[:, :, :], ALU.add).then_inc(s_y, 1)

            rstd(0, s_ve1, s_rs1, sm1)
            with pool.Fori(0, B - 1) as i:
                rstd(i, s_ve2, s_rs2, sm2)
                sum_experts(i, True)
            rstd(B - 1, s_ve2, s_rs2, sm2)
            sum_experts(B - 1, False)

        @block.tensor
        def _(pe):
            def take(part, name, i):
                k, _, before = place(part, name, i)
                if before:
                    pe.wait_ge(*release(*before))
                return ring[:, k]

            def flat(buf):
                return buf.rearrange("p a n -> p (a n)")

            def project(part, i, b):
                for which, name in ((0, "q"), (1, "k")):
                    buf = take(part, name, i)
                    if which == 0:
                        pe.wait_ge(s_xs, b + 1)
                    for h in range(2):
                        rows = xst[:, h * CHUNK:(h + 1) * CHUNK]
                        pe.matmul(buf[0:ROW, h, :], w1[:, which].rearrange("p r m -> p (r m)"), rows, start=True, stop=False)
                        mm = pe.matmul(buf[0:ROW, h, :], w2[:, which].rearrange("p r m -> p (r m)"), rows, start=False, stop=True)
                    mm.then_inc(s_fill, 1)
                buf = take(part, "vx", i)
                for tile in range(T):
                    toks = xst[:, col(tile):col(tile) + P]
                    o = (tile % 4) * (M + C)
                    pe.matmul(buf[:, tile // 4, o:o + M + C], toks, vx1[:, :], start=True, stop=False)
                    mm = pe.matmul(buf[:, tile // 4, o:o + M + C], toks, vx2[:, :], start=False, stop=True)
                mm.then_inc(s_fill, 1)

            def max_scores(part, i, b, tile):
                buf = take(part, f"mx{tile}", i)
                if tile == 0:
                    pe.wait_ge(s_qks, 2 * (b + 1))
                for h in range(2):
                    mm = pe.matmul(buf[:, h, :], kst[0:ROW, col(tile):col(tile) + P], qst[0:ROW, h * CHUNK:(h + 1) * CHUNK],
                                   start=True, stop=True)
                mm.then_inc(s_fill, 1)

            def max_row(part, i, b):
                buf = take(part, "mrow", i)
                pe.wait_ge(s_nm, 2 * (b + 1))
                for tile in range(T):
                    c = col(tile)
                    mm = pe.matmul(flat(buf)[0:ROW + 2, c:c + P], nmax[:, tile, :], ident_r[:, :], start=True, stop=True)
                mm.then_inc(s_fill, 1)

            def scores1(part, i, b, j):
                buf = take(part, f"st{j}", i)
                if j == 0:
                    pe.wait_ge(s_mrow, b + 1)
                for h in range(2):
                    mm = pe.matmul(buf[:, h, :], qst[0:ROW + 2, col(j):col(j) + P], kst[0:ROW + 2, h * CHUNK:(h + 1) * CHUNK],
                                   start=True, stop=True)
                mm.then_inc(s_fill, 1)

            def weigh(acc, stationary, prob, j, s_p, s_sum, b):
                pe.wait_ge(s_p, T * b + j + 1)
                for h in range(2):
                    mm = pe.matmul(acc[h * C:(h + 1) * C, :], stationary[:, j, :], prob[:, j % 2, h * CHUNK:(h + 1) * CHUNK],
                                   start=(j == 0), stop=(j == T - 1))
                if j == T - 1:
                    mm.then_inc(s_sum, 1)

            def project_out(part, i, b):
                buf = take(part, "po", i)
                pe.wait_ge(s_agg, b + 1)
                for t in range(4):
                    o = (t % 2) * 2 * (C + 1)
                    mm = pe.matmul(buf[:, t // 2, o:o + 2 * (C + 1)], agg[:, t * P:(t + 1) * P],
                                   wo_blk[:, :, :].rearrange("p h c -> p (h c)"), start=True, stop=True)
                mm.then_inc(s_fill, 1)

            def u_transposed(part, i, b):
                buf = take(part, "uT", i)
                pe.wait_ge(s_u, b + 1)
                for which in range(2):
                    half_buf = buf[:, which, :].bitcast(F16)
                    for tile in range(T):
                        c = col(tile)
                        mm = pe.transpose(half_buf[:, c:c + P], uhl[:, tile, which:which + 2, :].rearrange("p a c -> p (a c)"),
                                          ident_h[:, :])
                mm.then_inc(s_fill, 1)

            def scores2(part, i, b, j):
                buf = take(part, f"s{j}", i)
                if j == 0:
                    pe.wait_ge(s_z, 2 * (b + 1))
                z = zst[:, col(j):col(j) + P]
                for h in range(2):
                    pe.matmul(buf[:, h, :], z, zst[:, h * CHUNK:(h + 1) * CHUNK], start=True, stop=False)
                    mm = pe.matmul(buf[:, h, :], z, zsw[:, h * CHUNK:(h + 1) * CHUNK], start=False, stop=True)
                mm.then_inc(s_fill, 1)

            y_flat = y[:, :, :].rearrange("p t c -> p (t c)")

            def back_transposed(part, i, name, src, s_src, value):
                buf = take(part, name, i)
                pe.wait_ge(s_src, value)
                for t in range(4):
                    mm = pe.transpose(buf[:, 0, t * P:(t + 1) * P], src[:, t * P:(t + 1) * P], ident[:, :])
                mm.then_inc(s_fill, 1)

            def w_transposed(part, i, b):
                buf = take(part, "wT", i)
                pe.wait_ge(s_w, b + 1)
                for tile in range(T):
                    c = col(tile)
                    mm = pe.transpose(flat(buf)[:, c:c + P], wdup[:, tile].rearrange("p a c -> p (a c)"), ident[:, :])
                mm.then_inc(s_fill, 1)

            def route(part, i, b):
                buf = take(part, "rt", i)
                pe.wait_ge(s_ws, b + 1)
                for tile in range(T):
                    toks = wst[:, col(tile):col(tile) + P]
                    pe.matmul(buf[:, 0, tile * E:(tile + 1) * E], toks, r1[:, :], start=True, stop=False)
                    mm = pe.matmul(buf[:, 0, tile * E:(tile + 1) * E], toks, r2[:, :], start=False, stop=True)
                mm.then_inc(s_fill, 1)

            def experts(part, i, b, g):
                buf = take(part, f"e{g}", i)
                for h in range(2):
                    toks = wst[:, col(2 * g + h):col(2 * g + h) + P]
                    pe.matmul(buf[:, h, :], toks, e1[:, :], start=True, stop=False)
                    mm = pe.matmul(buf[:, h, :], toks, e2[:, :], start=False, stop=True)
                mm.then_inc(s_fill, 1)

            def gates_transposed(part, i, b):
                buf = take(part, "gT", i)
                pe.wait_ge(s_gate, b + 1)
                pe.transpose(buf[:, 0, 0:P], gate[:, :, :].rearrange("p t e -> p (t e)"), ident[:, :]).then_inc(s_fill, 1)

            def expert_bias(b):
                pe.wait_ge(s_gt, b + 2)
                pe.matmul(acc2[:, :], gate_t[:, :], eb_blk[:, :, :].rearrange("p t c -> p (t c)"),
                          start=True, stop=True).then_inc(s_gb, 1)

            buf = take("first", "w3", 0)
            pe.wait_ge(s_const, 2)
            pe.wait_ge(s_w3, 6 * 16)
            pe.transpose(buf[:, 0, 0:ROW], w3[:, :, :].rearrange("p a c -> p (a c)"), ident[0:ROW, 0:ROW]).then_inc(s_fill, 1)
            buf = take("first", "wo", 0)
            pe.wait_ge(s_wol, 2 * 16)
            pe.transpose(buf[:, 0, 0:C], wo4[:, :, :].rearrange("p a m -> p (a m)"), ident[0:C, 0:C]).then_inc(s_fill, 1)
            pe.wait_ge(s_wts, 3)
            project("first", 0, 0)
            for tile in range(T):
                max_scores("first", 0, 0, tile)
            max_row("first", 0, 0)
            for j in range(T):
                scores1("first", 0, 0, j)
                if j:
                    weigh(acc1, val, prob1, j - 1, s_p1, s_av1, 0)
            weigh(acc1, val, prob1, T - 1, s_p1, s_av1, 0)
            pe.wait_ge(s_wblk, 2)
            project_out("first", 0, 0)
            pe.wait_ge(s_es, 3)
            for name in FIRST[-RING:]:
                pe.wait_ge(*release(name, "first", 0))

            with pe.Fori(0, B - 1) as i:
                project("body", i, i + 1)
                u_transposed("body", i, i)
                for j in range(T):
                    scores2("body", i, i, j)
                    if j:
                        weigh(acc2, u, prob2, j - 1, s_p2, s_av2, i)
                    for tile in MX_AT[j]:
                        max_scores("body", i, i + 1, tile)
                    if j == 3:
                        back_transposed("body", i, "yT-", y_flat, s_y, i + 1)
                max_row("body", i, i + 1)
                weigh(acc2, u, prob2, T - 1, s_p2, s_av2, i)
                for j in range(T):
                    scores1("body", i, i + 1, j)
                    if j:
                        weigh(acc1, val, prob1, j - 1, s_p1, s_av1, i + 1)
                    if j == 0:
                        back_transposed("body", i, "oT", att2, s_att2, i + 1)
                    if j == 3:
                        w_transposed("body", i, i)
                    if j == 5:
                        route("body", i, i)
                    if j == 6:
                        experts("body", i, i, 0)
                    if j == 7:
                        experts("body", i, i, 1)
                weigh(acc1, val, prob1, T - 1, s_p1, s_av1, i + 1)
                experts("body", i, i, 2)
                project_out("body", i, i + 1)
                gates_transposed("body", i, i)
                experts("body", i, i, 3)
                expert_bias(i)

            b = B - 1
            u_transposed("last", b, b)
            for j in range(T):
                scores2("last", b, b, j)
                if j:
                    weigh(acc2, u, prob2, j - 1, s_p2, s_av2, b)
                if j == 3:
                    back_transposed("last", b, "yT-", y_flat, s_y, b + 1)
            weigh(acc2, u, prob2, T - 1, s_p2, s_av2, b)
            back_transposed("last", b, "oT", att2, s_att2, b + 1)
            w_transposed("last", b, b)
            route("last", b, b)
            experts("last", b, b, 0)
            gates_transposed("last", b, b)
            experts("last", b, b, 1)
            expert_bias(b)
            experts("last", b, b, 2)
            experts("last", b, b, 3)
            back_transposed("last", b, "yT", y_flat, s_y, b + 2)

        @block.scalar
        def _(act):
            def filled(part, name, i):
                k, n, _ = place(part, name, i)
                act.wait_ge(s_fill, n + 1)
                return ring[:, k]

            def flat(buf):
                return buf.rearrange("p a n -> p (a n)")

            def round_x(slot):
                act.activation(xst[:, :], slot, ACT.Copy).then_inc(s_xr, 1)

            def round_qk(part, i):
                act.activation(qst[0:ROW, :], flat(filled(part, "q", i))[0:ROW, :], ACT.Copy).then_inc(s_qkr, 1)
                act.activation(kst[0:ROW, :], flat(filled(part, "k", i))[0:ROW, :], ACT.Copy).then_inc(s_qkr, 1)

            def values(part, i, b):
                buf = filled(part, "vx", i)
                b4 = buf[:, :, 0:4 * (M + C)].rearrange("p a (t c) -> p a t c", c=M + C)
                act.activation(val[:, :, 0:M].rearrange("p (a t) c -> p a t c", a=2), b4[:, :, :, 0:M],
                               ACT.Copy).then_inc(s_vx, 1)
                act.wait_ge(s_tk1, b)
                act.activation(xt[:, :, :].rearrange("p (a t) c -> p a t c", a=2), b4[:, :, :, M:M + C],
                               ACT.Copy).then_inc(s_vx, 1)

            def max_row(part, i):
                buf = filled(part, "mrow", i)
                act.activation(kst[ROW:ROW + 2, :], flat(buf)[ROW:ROW + 2, :], ACT.Copy).then_inc(s_mrow, 1)

            def exp1(part, i, j):
                act.activation(prob1[:, j % 2, :], flat(filled(part, f"st{j}", i)), ACT.Exp).then_inc(s_p1, 1)

            def exp2(part, i, j):
                act.activation(prob2[:, j % 2, :], flat(filled(part, f"s{j}", i)), ACT.Exp, bias=shift[:, :],
                               accum_out=rsum2[:, j:j + 1]).then_inc(s_p2, 1)

            def copy_sums(dst, src, s_sum, b, s_ready):
                act.wait_ge(s_sum, b + 1)
                act.activation(dst, src, ACT.Copy).then_inc(s_ready, 1)

            def stack_swapped(part, i):
                buf = filled(part, "uT", i)
                act.activation(zsw[:, :], buf[:, 1, :].bitcast(F16), ACT.Copy).then_inc(s_z, 1)

            def round_w(part, i):
                act.activation(wst[:, :], flat(filled(part, "wT", i)), ACT.Copy).then_inc(s_wr, 1)

            def gap_exp(b):
                act.wait_ge(s_gap, b + 1)
                act.activation(gm[:, 5, :], gm[:, 4, :], ACT.Exp).then_inc(s_eg, 1)

            def copy_gates(part, i):
                buf = filled(part, "gT", i)
                act.activation(gate_t[:, :], buf[0:T * E, 0, 0:P], ACT.Copy).then_inc(s_gt, 1)

            def result(part, name, i, image):
                buf = filled(part, name, i)
                act.wait_ge(s_ob_free, image + 1)
                act.activation(ob[:, :], buf[:, 0, :], ACT.Copy).then_inc(s_ob, 1)

            act.wait_ge(s_x[0], 32)
            act.wait_ge(s_const, 2)
            round_x(xin[:, 0, :])
            buf = filled("first", "w3", 0)
            for r in range(3):
                act.activation(w1[:, :, r, :], buf[:, 0, 0:2 * M].rearrange("p (a m) -> p a m", a=2), ACT.Copy).then_inc(s_wr1, 1)
            act.activation(vx1[:, 0:M], buf[:, 0, 2 * M:3 * M], ACT.Copy).then_inc(s_wr1, 1)
            round_qk("first", 0)
            values("first", 0, 0)
            act.wait_ge(s_x[1], 32)
            round_x(xin[:, 1, :])
            act.wait_ge(s_ew, (5 + T) * 16)
            act.activation(e1[:, :], e_in[:, :, :].rearrange("p e c -> p (e c)"), ACT.Copy).then_inc(s_er, 1)
            act.activation(r1[:, :], r_in[:, :], ACT.Copy).then_inc(s_er, 1)
            act.activation(gate_t[:, :], ident[0:T * E, :], ACT.Copy).then_inc(s_gt, 1)
            max_row("first", 0)
            for j in range(T):
                exp1("first", 0, j)
            copy_sums(agg[:, :], acc1[:, :], s_av1, 0, s_agg)
            for b in range(2, B):
                act.wait_ge(s_x[b], 32)

            with act.Fori(0, B - 1) as i:
                round_qk("body", i)
                values("body", i, i + 1)
                stack_swapped("body", i)
                for j in range(T):
                    exp2("body", i, j)
                    if j == 4:
                        result("body", "yT-", i, i)
                    if j == 5:
                        round_x(xin[:, bass.ds(i + 2, 1), :].rearrange("p a n -> p (a n)"))
                max_row("body", i)
                copy_sums(att2[:, :], acc2[:, :], s_av2, i, s_att2)
                for j in range(T):
                    exp1("body", i, j)
                    if j == 3:
                        round_w("body", i)
                    if j == 6:
                        gap_exp(i)
                copy_sums(agg[:, :], acc1[:, :], s_av1, i + 1, s_agg)
                copy_gates("body", i)
                copy_sums(ybias[:, :, :].rearrange("p t c -> p (t c)"), acc2[:, :], s_gb, i, s_gbs)

            b = B - 1
            stack_swapped("last", b)
            for j in range(T):
                exp2("last", b, j)
                if j == 4:
                    result("last", "yT-", b, b)
            copy_sums(att2[:, :], acc2[:, :], s_av2, b, s_att2)
            round_w("last", b)
            gap_exp(b)
            copy_gates("last", b)
            copy_sums(ybias[:, :, :].rearrange("p t c -> p (t c)"), acc2[:, :], s_gb, b, s_gbs)
            result("last", "yT", b, b + 1)

        @block.vector
        def _(dve):
            def filled(part, name, i):
                k, n, _ = place(part, name, i)
                dve.wait_ge(s_fill, n + 1)
                return ring[:, k]

            def flat(buf):
                return buf.rearrange("p a n -> p (a n)")

            def wide(a, n):
                return a.unsqueeze(2).to_broadcast([P, T, n])

            def split_x(b, slot):
                dve.wait_ge(s_xr, b + 1)
                lo = xst[C:P, :]
                dve.tensor_tensor(lo, slot, lo.bitcast(F32), ALU.subtract).then_inc(s_xs, 1)

            def split_q(part, i, b):
                buf = filled(part, "q", i)
                dve.wait_ge(s_qkr, 2 * b + 1)
                lo = qst[M:2 * M, :]
                dve.tensor_tensor(lo, flat(buf)[M:2 * M, :], lo.bitcast(F32), ALU.subtract).then_inc(s_qks, 1)

            def split_k(part, i, b):
                buf = filled(part, "k", i)
                dve.wait_ge(s_qkr, 2 * b + 2)
                lo = kst[2 * M:3 * M, :]
                dve.tensor_tensor(lo, flat(buf)[2 * M:3 * M, :], lo.bitcast(F32), ALU.subtract).then_inc(s_qks, 1)

            def row_max(part, i, tile):
                dve.tensor_reduce(rowmax[:, tile:tile + 1], flat(filled(part, f"mx{tile}", i)), AX.X, ALU.max).then_inc(s_mx, 1)

            def negate_max(b):
                dve.wait_ge(s_mx, T * (b + 1))
                hi = nmax[:, :, ROW:ROW + 1]
                rm = rowmax[:, :].unsqueeze(2)
                dve.tensor_scalar(hi, rm, -1.0, None, ALU.mult).then_inc(s_nm, 1)
                dve.wait_ge(s_nm, 2 * b + 1)
                dve.scalar_tensor_tensor(out=nmax[:, :, ROW + 1:ROW + 2], in0=rm, scalar=-1.0, in1=hi.bitcast(F32),
                                         op0=ALU.mult, op1=ALU.subtract).then_inc(s_nm, 1)

            def tokens1(part, i, b):
                buf = filled(part, "po", i)
                po = buf[:, :, 0:4 * (C + 1)].rearrange("p a (t c) -> p a t c", c=C + 1)
                r4 = rinv1[:, :].rearrange("p (a t) -> p a t", a=2).unsqueeze(3)
                dve.reciprocal(r4, po[:, :, :, C:C + 1]).then_inc(s_t1, 1)
                dve.wait_ge(s_t1, b + 1)
                dve.tensor_tensor(tdiv[:, :, :].rearrange("p (a t) c -> p a t c", a=2), po[:, :, :, 0:C],
                                  r4.to_broadcast([P, 2, 4, C]), ALU.mult).then_inc(s_po, 1)
                dve.wait_ge(s_po, b + 1)
                dve.wait_ge(s_vx, 2 * b + 2)
                dve.tensor_tensor(tok1[:, :, :], tdiv[:, :, :], xt[:, :, :], ALU.add).then_inc(s_tk1, 1)

            def norm_stats(tok, s_tok, stats, sm, s_ln, s_ve, b):
                dve.wait_ge(s_tok, b + 1)
                ln = Steps(dve, s_ln, 4, b)
                for tile in range(T):
                    last = dve.bn_stats(stats[:, tile, :], tok[:, tile, :])
                ln.then(last)
                mean_e, var_e, mean_o, var_o = (stats[:, :, k] for k in (1, 2, 4, 5))
                dve.tensor_tensor(sm[:, 0, :], mean_e, mean_o, ALU.subtract)
                dve.tensor_tensor(sm[:, 1, :], mean_e, mean_o, ALU.add)
                ln.then(dve.tensor_tensor(sm[:, 4, :], var_e, var_o, ALU.add))
                dve.tensor_scalar(sm[:, 1, :], sm[:, 1, :], -0.5, None, ALU.mult)
                ln.then(dve.scalar_tensor_tensor(out=sm[:, 5, :], in0=sm[:, 0, :], scalar=C / 4.0, in1=sm[:, 0, :],
                                                 op0=ALU.mult, op1=ALU.mult))
                ln.then(dve.tensor_tensor(sm[:, 4, :], sm[:, 4, :], sm[:, 5, :], ALU.add))
                ln.end()
                dve.tensor_scalar(sm[:, 2, :], sm[:, 4, :], 1.0 / C, EPS, ALU.mult, ALU.add).then_inc(s_ve, 1)

            def normalize1(b):
                dve.wait_ge(s_rs1, b + 1)
                for tile in range(T):
                    last = dve.tensor_scalar(u[:, tile, :], tok1[:, tile, :], sm1[:, 1, tile:tile + 1], sm1[:, 3, tile:tile + 1],
                                             ALU.add, ALU.mult)
                un = Steps(dve, s_un, 2, b)
                un.then(last)
                dve.tensor_copy(uhl[:, :, 0, :], u[:, :, :])
                un.then(dve.tensor_copy(uhl[:, :, 2, :], u[:, :, :]))
                un.end()
                dve.tensor_tensor(uhl[:, :, 1, :], u[:, :, :], uhl[:, :, 2, :], ALU.subtract).then_inc(s_u, 1)

            def stack_u(part, i):
                buf = filled(part, "uT", i)
                dve.tensor_copy(zst[:, :], buf[:, 0, :].bitcast(F16)).then_inc(s_z, 1)

            def tokens2(part, i, b):
                dve.wait_ge(s_p2, T * (b + 1))
                dve.reciprocal(rinv2[:, :], rsum2[:, :]).then_inc(s_t2, 1)
                buf = filled(part, "oT", i)
                dve.wait_ge(s_t2, b + 1)
                dve.tensor_tensor(odiv[:, :, :], buf[:, 0, :].rearrange("p (t c) -> p t c", c=C), wide(rinv2[:, :], C),
                                  ALU.mult).then_inc(s_oT, 1)
                dve.wait_ge(s_oT, b + 1)
                dve.tensor_tensor(tok2[:, :, :], odiv[:, :, :], tok1[:, :, :], ALU.add).then_inc(s_tk2, 1)

            def normalize2(b):
                dve.wait_ge(s_rs2, b + 1)
                for tile in range(T):
                    last = dve.tensor_scalar(wdup[:, tile, :, :], tok2[:, tile, :].unsqueeze(1).to_broadcast([P, 2, C]),
                                             sm2[:, 1, tile:tile + 1], sm2[:, 3, tile:tile + 1], ALU.add, ALU.mult)
                last.then_inc(s_w, 1)

            def split_w(part, i, b):
                buf = filled(part, "wT", i)
                dve.wait_ge(s_wr, b + 1)
                lo = wst[C:P, :]
                dve.tensor_tensor(lo, flat(buf)[C:P, :], lo.bitcast(F32), ALU.subtract).then_inc(s_ws, 1)

            def top2(part, i, b):
                buf = filled(part, "rt", i)
                dve.tensor_tensor(lg[:, :, :], buf[:, 0, 0:T * E].rearrange("p (t e) -> p t e", e=E),
                                  rb_all[:, :].unsqueeze(1).to_broadcast([P, T, E]), ALU.add).then_inc(s_lg, 1)
                dve.wait_ge(s_lg, b + 1)
                top = Steps(dve, s_top, 13, b)
                src = lg
                for n, pick in enumerate((pick1, pick2)):
                    top.then(dve.tensor_reduce(gm[:, 2 * n, :], src[:, :, :], AX.X, ALU.max))
                    top.then(dve.tensor_tensor(cand[:, :, :], src[:, :, :], wide(gm[:, 2 * n, :], E), ALU.is_equal))
                    top.then(dve.tensor_tensor(cand[:, :, :], cand[:, :, :], ramp[:, :, :], ALU.mult))
                    top.then(dve.tensor_reduce(gm[:, 2 * n + 1, :], cand[:, :, :], AX.X, ALU.max))
                    top.then(dve.tensor_tensor(pick[:, :, :], cand[:, :, :], wide(gm[:, 2 * n + 1, :], E), ALU.is_equal))
                    if n == 0:
                        top.then(dve.scalar_tensor_tensor(out=lg2[:, :, :], in0=pick1[:, :, :], scalar=LOWEST, in1=lg[:, :, :],
                                                          op0=ALU.mult, op1=ALU.add))
                        src = lg2
                    if n == 1:
                        dve.tensor_tensor(gm[:, 4, :], gm[:, 2, :], gm[:, 0, :], ALU.subtract).then_inc(s_gap, 1)
                dve.wait_ge(s_eg, b + 1)
                top.then(dve.tensor_scalar(gm[:, 6, :], gm[:, 5, :], 1.0, None, ALU.add))
                top.then(dve.reciprocal(gm[:, 6, :], gm[:, 6, :]))
                top.end()
                gt = Steps(dve, s_gs, 2, b)
                dve.tensor_tensor(pick1[:, :, :], pick1[:, :, :], wide(gm[:, 6, :], E), ALU.mult)
                gt.then(dve.tensor_tensor(gm[:, 7, :], gm[:, 5, :], gm[:, 6, :], ALU.mult))
                gt.then(dve.tensor_tensor(pick2[:, :, :], pick2[:, :, :], wide(gm[:, 7, :], E), ALU.mult))
                gt.end()
                dve.tensor_tensor(gate[:, 0:T, :], pick1[:, :, :], pick2[:, :, :], ALU.add).then_inc(s_gate, 1)

            def weigh_experts(part, i, b, g):
                buf = filled(part, f"e{g}", i)
                if g == 0:
                    dve.wait_ge(s_gate, b + 1)
                if g >= 2:
                    dve.wait_ge(s_half, (T // 2) * b + g - 1)
                gates = gate[:, 2 * g:2 * g + 2, :].rearrange("p t e -> p (t e)").unsqueeze(2).to_broadcast([P, 2 * E, C])
                dve.tensor_tensor(prod[:, g % 2].rearrange("p t e c -> p (t e) c"),
                                  flat(buf).rearrange("p (x c) -> p x c", c=C), gates, ALU.mult).then_inc(s_prod, 1)

            dve.wait_ge(s_const, 2)
            dve.tensor_copy(ident_r[:, :], ident[:, :])
            dve.tensor_tensor(vx1[:, M:M + C], ident[:, 0:C], ident[:, C:P], ALU.add).then_inc(s_wts, 1)
            dve.memset(qst[ROW:ROW + 2, :].bitcast(F32), 1.0)
            dve.memset(shift[:, :], -SHIFT).then_inc(s_shift, 1)
            split_x(0, xin[C:P, 0, :])
            buf = filled("first", "w3", 0)
            dve.wait_ge(s_wr1, 4)
            dve.tensor_tensor(w2[:, :, :, :], buf[:, 0, 0:2 * M].rearrange("p (a m) -> p a m", a=2).unsqueeze(2)
                              .to_broadcast([P, 2, 3, M]), w1[:, :, :, :].bitcast(F32), ALU.subtract).then_inc(s_wts, 1)
            dve.memset(vx2[:, M:M + C].bitcast(F32), 0.0)
            dve.tensor_tensor(vx2[:, 0:M], buf[:, 0, 2 * M:3 * M], vx1[:, 0:M].bitcast(F32), ALU.subtract).then_inc(s_wts, 1)
            buf = filled("first", "wo", 0)
            dve.wait_ge(s_const, 4)
            for h in range(2):
                dve.memset(wo_blk[h * C + ONE:h * C + ONE + 1, h, C:C + 1], 1.0)
                dve.tensor_copy(wo_blk[h * C:(h + 1) * C, h, 0:C], buf[h * C:(h + 1) * C, 0, 0:C]).then_inc(s_wblk, 1)
            dve.tensor_copy(ident_h[:, :], ident[:, :]).then_inc(s_prod, T // 2)
            split_q("first", 0, 0)
            split_k("first", 0, 0)
            for tile in range(T):
                row_max("first", 0, tile)
            negate_max(0)
            dve.wait_ge(s_fill, FIRST.index("vx") + 1)
            split_x(1, xin[C:P, 1, :])
            dve.wait_ge(s_er, 2)
            dve.tensor_tensor(e2[:, :], e_in[:, :, :].rearrange("p e c -> p (e c)"), e1[:, :].bitcast(F32),
                              ALU.subtract).then_inc(s_es, 1)
            dve.tensor_tensor(r2[:, :], r_in[:, :], r1[:, :].bitcast(F32), ALU.subtract).then_inc(s_es, 1)
            dve.wait_ge(s_const, 5)
            dve.tensor_tensor(eb_blk[:, :, :], eb_in[:, :].unsqueeze(1).to_broadcast([T * E, T, C]),
                              tile_mask[:, :].unsqueeze(2).to_broadcast([T * E, T, C]), ALU.mult).then_inc(s_es, 1)
            tokens1("first", 0, 0)
            norm_stats(tok1, s_tk1, stats1, sm1, s_ln1, s_ve1, 0)
            normalize1(0)

            with dve.Fori(0, B - 1) as i:
                split_q("body", i, i + 1)
                split_k("body", i, i + 1)
                stack_u("body", i)
                for tile in range(T):
                    row_max("body", i, tile)
                    if tile == 5:
                        split_x(i + 2, xin[C:P, bass.ds(i + 2, 1), :].rearrange("p a n -> p (a n)"))
                negate_max(i + 1)
                tokens2("body", i, i)
                norm_stats(tok2, s_tk2, stats2, sm2, s_ln2, s_ve2, i)
                normalize2(i)
                split_w("body", i, i)
                top2("body", i, i)
                for g in range(3):
                    weigh_experts("body", i, i, g)
                tokens1("body", i, i + 1)
                norm_stats(tok1, s_tk1, stats1, sm1, s_ln1, s_ve1, i + 1)
                weigh_experts("body", i, i, 3)
                normalize1(i + 1)

            b = B - 1
            stack_u("last", b)
            tokens2("last", b, b)
            norm_stats(tok2, s_tk2, stats2, sm2, s_ln2, s_ve2, b)
            normalize2(b)
            split_w("last", b, b)
            top2("last", b, b)
            for g in range(T // 2):
                weigh_experts("last", b, b, g)


_INS = ["x", "L0_conv_wq", "L0_conv_wk", "L0_conv_wv", "L0_conv_wo", "L1_ffn_router_w", "L1_ffn_router_b",
        "L1_ffn_expert_w", "L1_ffn_expert_b"]


def kernel(**inputs):
    import numpy as _np
    import concourse.bacc as _bacc
    from concourse import mybir as _mybir
    from concourse.bass_utils import run_bass_kernel_spmd as _run

    nc = _bacc.Bacc("TRN2", target_bir_lowering=False, num_devices=1)
    arrays, args = {}, []
    for name in _INS:
        a = _np.ascontiguousarray(inputs[name])
        arrays[f"in_{name}"] = a
        args.append(nc.dram_tensor(f"in_{name}", a.shape, _mybir.dt.from_np(a.dtype), kind="ExternalInput").ap())
    shape = inputs["x"].shape
    args.append(nc.dram_tensor("out_0", shape, _mybir.dt.float32, kind="ExternalOutput").ap())
    build(nc, *args)
    return _run(nc, [arrays], core_ids=[0]).results[0]["out_0"]
```

```python
from contextlib import ExitStack

import concourse.bass as bass
from concourse import mybir

ALU = mybir.AluOpType
ACT = mybir.ActivationFunctionType
AX = mybir.AxisListType
F32 = mybir.dt.float32
F32R = mybir.dt.float32r
F16 = mybir.dt.float16

P = 128
B, C, N, M, E = 4, 64, 1024, 32, 8
CHUNK = 512
T = N // P
EPS = 1e-5
ONE = M
ROW = 3 * M
ROOT_C = float(C) ** 0.5
SHIFT = float(C) / 2

RING = 3
WHOLE = [slice(0, 2)]
HALVES = [slice(0, 1), slice(1, 2)]
ON_POOL = [0, 2]
ON_VECTOR = 3
SUM_ORDER = [1, 0, 3, 2]
MX_AT = [[], [0, 1], [2, 3], [4], [5], [6], [7], []]
FIRST = (["w3", "wo", "q", "k", "vx"] + [f"mx{i}" for i in range(T)] + ["mrow"] + [f"st{j}" for j in range(T)]
         + ["q+", "k+", "po", "vx+"])
BODY = []
LAST = []
for j in range(T):
    BODY += [f"s{j}"] + [f"mx{i}" for i in MX_AT[j]] + {6: ["yT-"], 7: ["mrow"]}.get(j, [])
    LAST += [f"s{j}"] + ["yT-"] * (j == 6)
for j in range(T):
    BODY += [f"st{j}"] + {5: ["wT"], 7: ["rt"]}.get(j, [])
BODY = [(name, n % RING) for n, name in enumerate(BODY)]
BODY += [("q+", 1), ("k+", 2), ("po", 0), ("e0", 1), ("e1", 0), ("vx+", 2), ("e3", 2), ("e2", 1)]
LAST += ["wT2", "rt", "e0", "e1", "e2", "e3"]
LAST = [(name, n % RING) for n, name in enumerate(LAST)]
FIRST = [(name, n % RING) for n, name in enumerate(FIRST)]


def columns(piece):
    return slice(piece.start * CHUNK, piece.stop * CHUNK)


def use(uses, name):
    return [n for n, _ in uses].index(name)


def last_use(uses, buf):
    return ([n for n, b in uses if b == buf] or [None])[-1]


def col(tile):
    return (tile % 2) * CHUNK + (tile // 2) * P


def build(nc, x, wq, wk, wv, wo, rw, rb, ew, eb, out):
    ctx = ExitStack()
    with ctx:
        def sb(name, shape, dt=F32):
            return ctx.enter_context(nc.sbuf_tensor(name, shape, dt))

        def sem(name):
            return ctx.enter_context(nc.semaphore(name))

        ident = sb("ident", [P, P])
        ident_h = sb("ident_h", [P, P], F16)
        ident_r = sb("ident_r", [P, P], F32R)
        filler = sb("filler", [P, CHUNK], F16)
        minus_half = sb("minus_half", [P, T])
        shift = sb("shift", [P, 1])
        ramp = sb("ramp", [P, T, E])
        w3 = sb("w3", [ROW, 2, C])
        wo4 = sb("wo4", [C, 4, M])
        w1 = sb("w1", [P, 2, 3, M], F32R)
        w2 = sb("w2", [P, 2, 3, M], F32R)
        vx1 = sb("vx1", [P, M + C], F32R)
        vx2 = sb("vx2", [P, M + C], F32R)
        wo_blk = sb("wo_blk", [P, 2, C + 1])
        e_in = sb("e_in", [P, E, C])
        e1 = sb("e1", [P, E * C], F32R)
        e2 = sb("e2", [P, E * C], F32R)
        r_in = sb("r_in", [P, E])
        r12 = sb("r12", [P, 2, E], F32R)
        rb_all = sb("rb_all", [P, E])
        eb_in = sb("eb_in", [T * E, C])
        eb_blk = sb("eb_blk", [T * E, T, C])
        tile_mask = sb("tile_mask", [T * E, T])

        xin = sb("xin", [P, B + 1, N])
        xst = sb("xst", [P, N], F32R)
        qst = sb("qst", [P, N], F32R)
        kst = sb("kst", [P, N], F32R)
        qk_f = sb("qk_f", [P, N])
        val = sb("val", [P, T, C])
        xt = sb("xt", [P, T, C])
        rowmax = sb("rowmax", [P, T])
        nmax = sb("nmax", [P, T, ROW + 2], F32R)
        nmax_f = sb("nmax_f", [P, T])
        prob1 = sb("prob1", [P, 2, N])
        prob2 = sb("prob2", [P, 2, N])
        agg = sb("agg", [P, CHUNK])
        rinv1 = sb("rinv1", [P, T])
        tok1 = sb("tok1", [P, T, C])
        tdiv = sb("tdiv", [P, T, C])
        stats1 = sb("stats1", [P, T, 6])
        sm1 = sb("sm1", [P, 7, T])
        cen1 = sb("cen1", [P, T, C])
        u = sb("u", [P, T, C])
        uhl = sb("uhl", [P, T, 3, C], F16)
        zst = sb("zst", [P, N], F16)
        zsw = sb("zsw", [P, N], F16)
        rsum2 = sb("rsum2", [P, T])
        rinv2 = sb("rinv2", [P, T])
        att2 = sb("att2", [P, CHUNK])
        tok2 = sb("tok2", [P, T, C])
        odiv = sb("odiv", [P, T, C])
        stats2 = sb("stats2", [P, T, 6])
        sm2 = sb("sm2", [P, 7, T])
        cen2 = sb("cen2", [P, T, C])
        wdup = sb("wdup", [P, T, 2, C])
        wst = sb("wst", [P, N], F32R)
        lg_1 = sb("lg_1", [P, T, E])
        lg = sb("lg", [P, T, E])
        top8 = sb("top8", [P, T, E])
        cand = sb("cand", [P, 2, T, E])
        cand2 = sb("cand2", [P, T, E])
        landing = sb("landing", [P, 1])
        pick1 = sb("pick1", [P, T, E])
        pick2 = sb("pick2", [P, T, E])
        gm = sb("gm", [P, 7, T])
        gate = sb("gate", [P, 2 * T, E])
        gate_t = sb("gate_t", [T * E, P])
        prod = sb("prod", [P, T // 2, E, 2, C])
        half = sb("half", [P, E // 2, 2, C])
        quart = sb("quart", [P, E // 4, 2, C])
        ysum = sb("ysum", [P, T, C])
        ybias = sb("ybias", [P, T, C])
        yres = sb("yres", [P, T, C])
        y = sb("y", [P, T, C])
        ob = sb("ob", [P, CHUNK])

        ring = ctx.enter_context(nc.psum_tensor("ring", [P, RING, 2, CHUNK], F32))
        acc1 = ctx.enter_context(nc.psum_tensor("acc1", [P, CHUNK], F32))
        acc2 = ctx.enter_context(nc.psum_tensor("acc2", [P, CHUNK], F32))

        s_fill = sem("ring_filled")
        s_const = sem("const_ready")
        s_filler = sem("filler_ready")
        s_pool = sem("pool_step")
        s_shift = sem("shift_ready")
        s_w3 = sem("w3_loaded")
        s_wol = sem("wo_loaded")
        s_ew = sem("experts_loaded")
        s_x = [sem(f"x_loaded{b}") for b in range(B)]
        s_wr1 = sem("weights_rounded")
        s_wts = sem("weights_split")
        s_wblk = sem("wo_blk_ready")
        s_er = sem("experts_rounded")
        s_es = sem("experts_split")
        s_xr = sem("x_rounded")
        s_xs = sem("x_split")
        s_qr = sem("q_rounded")
        s_kr = sem("k_rounded")
        s_qf = sem("q_copied")
        s_kf = sem("k_copied")
        s_qks = sem("qk_split")
        s_vx = sem("v_and_x_ready")
        s_mx = sem("rowmax_ready")
        s_nm = sem("negmax_split")
        s_mrow = sem("maxrow_ready")
        s_p1 = sem("probs1_ready")
        s_av1 = sem("agg_summed")
        s_agg = sem("agg_ready")
        s_po = sem("projection_read")
        s_t1 = sem("tok1_step")
        s_tk1 = sem("tok1_ready")
        s_ln1 = sem("ln1_step")
        s_ve1 = sem("var1_ready")
        s_cen1 = sem("centered1_ready")
        s_rs1 = sem("rstd1_ready")
        s_un = sem("u_step")
        s_uh1 = sem("u_high_ready")
        s_uh = sem("u_high_copied")
        s_u = sem("uhl_ready")
        s_uT = sem("u_transposed")
        s_z = sem("z_ready")
        s_p2 = sem("probs2_ready")
        s_av2 = sem("att2_summed")
        s_att2 = sem("att2_ready")
        s_o = sem("att2_turned")
        s_oT = sem("att2_read")
        s_t2 = sem("rinv2_ready")
        s_tk2 = sem("tok2_ready")
        s_ln2 = sem("ln2_step")
        s_ve2 = sem("var2_ready")
        s_cen2 = sem("centered2_ready")
        s_rs2 = sem("rstd2_ready")
        s_wT = sem("w_transposed")
        s_w = sem("w_ready")
        s_wr = sem("w_rounded")
        s_ws = sem("w_split")
        s_lg1 = sem("logits_first_part")
        s_lg = sem("logits_ready")
        s_top = sem("top2_step")
        s_gap = sem("logit_gap_ready")
        s_eg = sem("gap_exp_ready")
        s_gate = sem("gates_ready")
        s_gT = sem("gates_turned")
        s_gt = sem("gates_transposed")
        s_gb = sem("expert_bias_summed")
        s_gbs = sem("ybias_ready")
        s_prod = sem("prods_ready")
        s_half = sem("prods_used")
        s_tree = sem("tree_step")
        s_tail = sem("last_experts_summed")
        s_tail_v = sem("last_experts_summed_v")
        s_yT = sem("last_y_turned")
        s_y = sem("y_ready")
        s_ob = sem("out_ready")
        s_out = sem("out_stored")
        s_ob_free = sem("ob_free")

        RELEASE = {"w3": (s_wts, 3, 3), "wo": (s_wblk, 2, 2), "q": (s_qks, 2, 1), "k": (s_qks, 2, 2), "vx": (s_vx, 2, 2),
                   "q+": (s_qf, 1, 1), "k+": (s_kf, 1, 1), "vx+": (s_vx, 2, 4),
                   "mrow": (s_mrow, 2, 2), "po": (s_po, 1, 1),
                   "wT": (s_ws, 1, 1), "wT2": (s_ws, 1, 2), "rt": (s_lg, 1, 1), "yT-": (s_ob, 1, 2)}
        RELEASE.update({f"mx{i}": (s_mx, T, i + 1) for i in range(T)})
        RELEASE.update({f"st{j}": (s_p1, T, j + 1) for j in range(T)})
        RELEASE.update({f"s{j}": (s_p2, T, j + 1) for j in range(T)})
        RELEASE.update({f"e{g}": (s_prod, T // 2, T // 2 + g + 1) for g in range(T // 2)})
        NEXT = {"q+", "k+", "vx+", "mrow", "po"} | {f"mx{i}" for i in range(T)} | {f"st{j}" for j in range(T)}

        def release(name, part, i):
            s, per, at = RELEASE[name]
            image = i + (part == "body" and name in NEXT) - (name == "yT-")
            return s, image * per + at

        def place(part, name, i):
            uses = {"first": FIRST, "body": BODY, "last": LAST}[part]
            idx = use(uses, name)
            k = uses[idx][1]
            before = last_use(uses[:idx], k)
            if part == "first":
                return k, idx, (before, "first", 0) if before else None
            if part == "body":
                before = (before, "body", i) if before else (last_use(BODY, k), "body", i - 1)
                return k, len(FIRST) + i * len(BODY) + idx, before
            before = (before, "last", B - 1) if before else (last_use(BODY, k), "body", B - 2)
            return k, len(FIRST) + (B - 1) * len(BODY) + idx, before

        class Steps:

            def __init__(self, engine, s, per_image, b):
                self.engine, self.s, self.per, self.base, self.n = engine, s, per_image, b * per_image, 0

            def then(self, instruction):
                self.n += 1
                instruction.then_inc(self.s, 1)
                self.engine.wait_ge(self.s, self.base + self.n)

            def end(self):
                assert self.n == self.per, (self.n, self.per)

        block = ctx.enter_context(nc.Block())

        @block.sync
        def _(sp):
            def load_x(b):
                for h in range(2):
                    sp.dma_start(xin[h * C:(h + 1) * C, b, :], x[b].rearrange("c h w -> c (h w)")).then_inc(s_x[b], 16)

            load_x(0)
            for n, w in enumerate((wq, wk, wv)):
                sp.dma_start(w3[n * M:(n + 1) * M, :, :], w.unsqueeze(1).to_broadcast([M, 2, C])).then_inc(s_w3, 16)
            sp.wait_ge(s_const, 1)
            for h in range(2):
                sp.dma_start(wo4[:, 2 * h, :], wo).then_inc(s_wol, 16)
            load_x(1)
            for h in range(2):
                sp.dma_start(e_in[h * C:(h + 1) * C, :, :], ew.rearrange("e d c -> d e c")).then_inc(s_ew, 16)
                sp.dma_start(r_in[h * C:(h + 1) * C, :], rw).then_inc(s_ew, 16)
            sp.dma_start(rb_all[:, :], rb.rearrange("(a e) -> a e", a=1).to_broadcast([P, E])).then_inc(s_ew, 16)
            for t in range(T):
                sp.dma_start(eb_in[t * E:(t + 1) * E, :], eb).then_inc(s_ew, 16)
            for b in range(2, B):
                load_x(b)

            def store(b, image):
                sp.wait_ge(s_ob, b + 2)
                for h in range(2):
                    sp.dma_start(image[:, h * CHUNK:(h + 1) * CHUNK], ob[h * C:(h + 1) * C, :]).then_inc(s_out, 16)
                sp.wait_ge(s_out, 2 * 16 * (b + 1))
                sp.sem_inc(s_ob_free, 1)

            flat = out.rearrange("b c h w -> (b c) (h w)")
            sp.sem_inc(s_ob_free, 2)
            with sp.Fori(0, B - 1) as i:
                store(i, flat[bass.ds(i * C, C), :])
            for half_sum in range(2):
                sp.wait_ge(s_ob, B + 1 + half_sum)
                lo, hi = half_sum * CHUNK // 2, (half_sum + 1) * CHUNK // 2
                for h in range(2):
                    sp.dma_start(flat[(B - 1) * C:B * C, h * CHUNK + lo:h * CHUNK + hi], ob[h * C:(h + 1) * C, lo:hi]).then_inc(s_out, 16)
            sp.wait_ge(s_out, 2 * 16 * (B + 1))

        @block.gpsimd
        def _(pool):
            pool.memset(wo4[:, :, :], 0.0).then_inc(s_const, 1)
            pool.memset(ident[:, :], 0.0).then_inc(s_pool, 1)
            pool.wait_ge(s_pool, 1)
            pool.affine_select(out=ident[:, :], in_=ident[:, :], compare_op=ALU.not_equal, fill=1.0, base=0,
                               pattern=[[-1, P]], channel_multiplier=1).then_inc(s_const, 1)
            pool.memset(nmax[:, :, :].bitcast(F32), 0.0)
            pool.memset(val[:, :, M + 1:C], 0.0)
            pool.memset(val[:, :, ONE:ONE + 1], 1.0).then_inc(s_const, 1)
            pool.memset(wo_blk[:, :, :], 0.0).then_inc(s_const, 1)
            pool.memset(minus_half[:, :], -0.5).then_inc(s_half, T // 2)
            pool.memset(y[:, :, :], 0.0).then_inc(s_y, 1)
            pool.memset(gate[:, T:2 * T, :], 0.0).then_inc(s_gbs, 1)
            pool.memset(xin[:, B, :], 0.0).then_inc(s_prod, T // 2)
            for e in range(E):
                last = pool.memset(ramp[:, :, e:e + 1], float(E - e))
            pool.memset(tile_mask[:, :], 1.0).then_inc(s_pool, 1)
            pool.wait_ge(s_pool, 2)
            pool.affine_select(out=tile_mask[:, :], in_=tile_mask[:, :], compare_op=ALU.is_ge, fill=0.0, base=0,
                               pattern=[[-E, T]], channel_multiplier=1).then_inc(s_pool, 1)
            pool.wait_ge(s_pool, 3)
            pool.affine_select(out=tile_mask[:, :], in_=tile_mask[:, :], compare_op=ALU.is_ge, fill=0.0, base=E - 1,
                               pattern=[[E, T]], channel_multiplier=-1).then_inc(s_const, 1)

            def rstd(b, s_ve, s_rs, sm):
                pool.wait_ge(s_ve, b + 1)
                pool.tensor_tensor(sm[:, 3, :], sm[:, 2, :], minus_half[:, :], ALU.pow).then_inc(s_rs, 1)

            def split_x(b, slot):
                pool.wait_ge(s_xr, b + 1)
                first = xst[C:P, :]
                pool.tensor_tensor(first, slot, first.bitcast(F32), ALU.subtract).then_inc(s_xs, 1)
                pool.wait_ge(s_xs, b + 1)

            def split_qk(b):
                pool.wait_ge(s_qf, b)
                first = qst[M:2 * M, :]
                pool.tensor_tensor(first, qk_f[M:2 * M, :], first.bitcast(F32), ALU.subtract).then_inc(s_qks, 1)
                pool.wait_ge(s_qks, 2 * b + 1)
                pool.wait_ge(s_kf, b)
                first = kst[2 * M:3 * M, :]
                pool.tensor_tensor(first, qk_f[2 * M:3 * M, :], first.bitcast(F32), ALU.subtract).then_inc(s_qks, 1)
                pool.wait_ge(s_qks, 2 * b + 2)

            def sum_pair(b, g, tree):
                pool.wait_ge(s_prod, (T // 2) * (b + 1) + g + 1)
                p = prod[:, g]
                pool.tensor_tensor(half[:, :, :, :], p[:, 0:E // 2], p[:, E // 2:E], ALU.add).then_inc(s_half, 1)
                pool.wait_ge(s_half, (T // 2) * (b + 1) + g + 1)
                tree.then(pool.tensor_tensor(quart[:, :, :, :], half[:, 0:E // 4], half[:, E // 4:E // 2], ALU.add))
                tree.then(pool.tensor_tensor(ysum[:, 2 * g:2 * g + 2, :], quart[:, 0], quart[:, 1], ALU.add))

            def residual(b, tree):
                tree.then(pool.tensor_tensor(yres[:, :, :], ysum[:, :, :], tok2[:, :, :], ALU.add))
                pool.wait_ge(s_gbs, b + 2)
                pool.tensor_tensor(y[:, :, :], yres[:, :, :], ybias[:, :, :], ALU.add).then_inc(s_y, 1)

            pool.wait_ge(s_const, 5)
            split_x(1, xin[C:P, 1, :])
            rstd(0, s_ve1, s_rs1, sm1)
            pool.wait_ge(s_rs1, 1)
            split_qk(1)
            with pool.Fori(0, B - 1) as i:
                pool.wait_ge(s_y, i + 1)
                split_x(i + 2, xin[C:P, bass.ds(i + 2, 1), :].rearrange("p a n -> p (a n)"))
                rstd(i, s_ve2, s_rs2, sm2)
                rstd(i + 1, s_ve1, s_rs1, sm1)
                tree = Steps(pool, s_tree, 2 * (T // 2) + 1, i)
                sum_pair(i, 0, tree)
                split_qk(i + 2)
                for g in range(1, T // 2):
                    sum_pair(i, g, tree)
                residual(i, tree)
                tree.end()
            b = B - 1
            rstd(b, s_ve2, s_rs2, sm2)
            for n, g in enumerate(ON_POOL):
                pool.wait_ge(s_prod, (T // 2) * (b + 1) + g + 1)
                pool.tensor_tensor(half[:, :, :, :], prod[:, g, 0:E // 2], prod[:, g, E // 2:E], ALU.add).then_inc(s_half, 1)
                pool.wait_ge(s_half, (T // 2) * (b + 1) + n + 1)
                pool.tensor_tensor(quart[:, :, :, :], half[:, 0:E // 4], half[:, E // 4:E // 2], ALU.add).then_inc(s_tree, 1)
                pool.wait_ge(s_tree, b * (2 * (T // 2) + 1) + n + 1)
                pool.tensor_tensor(ysum[:, 2 * g:2 * g + 2, :], quart[:, 0], quart[:, 1], ALU.add).then_inc(s_tail, 1)
                pool.wait_ge(s_tail, n + 1)

        @block.tensor
        def _(pe):
            def take(part, name, i):
                k, _, before = place(part, name, i)
                if before:
                    pe.wait_ge(*release(*before))
                return ring[:, k]

            def flat(buf):
                return buf.rearrange("p a n -> p (a n)")

            def project_qk(part, i, b, which, name):
                buf = take(part, name, i)
                if which == 0:
                    pe.wait_ge(s_xs, b + 1)
                for h in range(2):
                    rows = xst[:, h * CHUNK:(h + 1) * CHUNK]
                    pe.matmul(buf[0:ROW, h, :], w1[:, which].rearrange("p r m -> p (r m)"), rows, start=True, stop=False)
                    mm = pe.matmul(buf[0:ROW, h, :], w2[:, which].rearrange("p r m -> p (r m)"), rows, start=False, stop=True)
                mm.then_inc(s_fill, 1)

            def project_v(part, i, name):
                buf = take(part, name, i)
                for tile in range(T):
                    toks = xst[:, col(tile):col(tile) + P]
                    o = (tile % 4) * (M + C)
                    pe.matmul(buf[:, tile // 4, o:o + M + C], toks, vx1[:, :], start=True, stop=False)
                    mm = pe.matmul(buf[:, tile // 4, o:o + M + C], toks, vx2[:, :], start=False, stop=True)
                mm.then_inc(s_fill, 1)

            def max_scores(part, i, b, tile):
                buf = take(part, f"mx{tile}", i)
                if tile == 0:
                    pe.wait_ge(s_qks, 2 * (b + 1))
                for h in range(2):
                    mm = pe.matmul(buf[:, h, :], kst[0:ROW, col(tile):col(tile) + P], qst[0:ROW, h * CHUNK:(h + 1) * CHUNK],
                                   start=True, stop=True)
                mm.then_inc(s_fill, 1)

            def max_row(part, i, b):
                buf = take(part, "mrow", i)
                pe.wait_ge(s_nm, 2 * (b + 1))
                for tile in range(T):
                    c = col(tile)
                    mm = pe.matmul(flat(buf)[0:ROW + 2, c:c + P], nmax[:, tile, :], ident_r[:, :], start=True, stop=True)
                mm.then_inc(s_fill, 1)

            def scores1(part, i, b, j):
                buf = take(part, f"st{j}", i)
                if j == 0:
                    pe.wait_ge(s_mrow, 2 * (b + 1))
                for h in range(2):
                    mm = pe.matmul(buf[:, h, :], qst[0:ROW + 2, col(j):col(j) + P], kst[0:ROW + 2, h * CHUNK:(h + 1) * CHUNK],
                                   start=True, stop=True)
                mm.then_inc(s_fill, 1)

            def weigh(acc, stationary, prob, j, s_p, s_sum, b):
                pe.wait_ge(s_p, T * b + j + 1)
                for h in range(2):
                    mm = pe.matmul(acc[h * C:(h + 1) * C, :], stationary[:, j, :], prob[:, j % 2, h * CHUNK:(h + 1) * CHUNK],
                                   start=(j == 0), stop=(j == T - 1))
                if j == T - 1:
                    mm.then_inc(s_sum, 1)

            def project_out(part, i, b):
                buf = take(part, "po", i)
                pe.wait_ge(s_agg, b + 1)
                for t in range(4):
                    o = (t % 2) * 2 * (C + 1)
                    mm = pe.matmul(buf[:, t // 2, o:o + 2 * (C + 1)], agg[:, t * P:(t + 1) * P],
                                   wo_blk[:, :, :].rearrange("p h c -> p (h c)"), start=True, stop=True)
                mm.then_inc(s_fill, 1)

            def u_transposed(b):
                pe.wait_ge(s_gbs, b + 1)
                pe.wait_ge(s_uh, b + 1)
                pe.wait_ge(s_u, b + 1)
                for which, bank in enumerate((acc1, acc2)):
                    for tile in range(T):
                        c = col(tile)
                        mm = pe.transpose(bank[:, :].bitcast(F16)[:, c:c + P],
                                          uhl[:, tile, which:which + 2, :].rearrange("p a c -> p (a c)"), ident_h[:, :])
                    mm.then_inc(s_uT, 1)

            def scores2(part, i, b, j):
                buf = take(part, f"s{j}", i)
                if j == 0:
                    pe.wait_ge(s_z, 2 * (b + 1))
                z = zst[:, col(j):col(j) + P]
                for h in range(2):
                    pe.matmul(buf[:, h, :], z, zst[:, h * CHUNK:(h + 1) * CHUNK], start=True, stop=False)
                    mm = pe.matmul(buf[:, h, :], z, zsw[:, h * CHUNK:(h + 1) * CHUNK], start=False, stop=True)
                mm.then_inc(s_fill, 1)

            y_flat = y[:, :, :].rearrange("p t c -> p (t c)")

            def back_transposed(part, i, name, src, s_src, value):
                buf = take(part, name, i)
                pe.wait_ge(s_src, value)
                for t in range(4):
                    mm = pe.transpose(buf[:, 0, t * P:(t + 1) * P], src[:, t * P:(t + 1) * P], ident[:, :])
                mm.then_inc(s_fill, 1)

            def att2_transposed(b):
                pe.wait_ge(s_att2, b + 1)
                for t in range(4):
                    mm = pe.transpose(acc2[:, t * P:(t + 1) * P], att2[:, t * P:(t + 1) * P], ident[:, :])
                mm.then_inc(s_o, 1)

            def w_transposed(part, i, b, pieces):
                buf = take(part, "wT" if part == "body" else "wT2", i)
                for n, piece in enumerate(pieces):
                    pe.wait_ge(s_w, b + n + 1)
                    for tile in [tile for tile in range(T) if piece.start <= tile % 2 < piece.stop]:
                        c = col(tile)
                        mm = pe.transpose(flat(buf)[:, c:c + P], wdup[:, tile].rearrange("p a c -> p (a c)"), ident[:, :])
                    mm.then_inc(s_fill if n == len(pieces) - 1 else s_wT, 1)

            def route(part, i, b):
                buf = take(part, "rt", i)
                pe.wait_ge(s_ws, b + (1 if part == "body" else len(HALVES)))
                for tile in range(T):
                    toks = wst[:, col(tile):col(tile) + P]
                    mm = pe.matmul(buf[:, 0, tile * 2 * E:(tile + 1) * 2 * E], toks, r12[:, :, :].rearrange("p a e -> p (a e)"),
                                   start=True, stop=True)
                mm.then_inc(s_fill, 1)

            def experts(part, i, b, g):
                buf = take(part, f"e{g}", i)
                for h in range(2):
                    toks = wst[:, col(2 * g + h):col(2 * g + h) + P]
                    pe.matmul(buf[:, h, :], toks, e1[:, :], start=True, stop=False)
                    mm = pe.matmul(buf[:, h, :], toks, e2[:, :], start=False, stop=True)
                mm.then_inc(s_fill, 1)

            def gates_transposed(b):
                pe.wait_ge(s_oT, b + 1)
                pe.wait_ge(s_gate, b + 1)
                pe.transpose(acc2[:, 0:P], gate[:, :, :].rearrange("p t e -> p (t e)"), ident[:, :]).then_inc(s_gT, 1)

            def expert_bias(b):
                pe.wait_ge(s_gt, b + 1)
                pe.matmul(acc2[:, :], gate_t[:, :], eb_blk[:, :, :].rearrange("p t c -> p (t c)"),
                          start=True, stop=True).then_inc(s_gb, 1)

            def keep_clock(n):
                for _ in range(n):
                    pe.matmul(acc1[:, :], filler[:, 0:P], filler[:, :], start=True, stop=True)

            pe.wait_ge(s_filler, 1)
            keep_clock(9)
            buf = take("first", "w3", 0)
            pe.wait_ge(s_const, 2)
            pe.wait_ge(s_w3, 3 * 16)
            pe.transpose(buf[:, 0, 0:ROW], w3[:, :, :].rearrange("p a c -> p (a c)"), ident[0:ROW, 0:ROW]).then_inc(s_fill, 1)
            buf = take("first", "wo", 0)
            pe.wait_ge(s_wol, 2 * 16)
            pe.transpose(buf[:, 0, 0:C], wo4[:, :, :].rearrange("p a m -> p (a m)"), ident[0:C, 0:C]).then_inc(s_fill, 1)
            keep_clock(3)
            pe.wait_ge(s_wts, 3)
            project_qk("first", 0, 0, 0, "q")
            project_qk("first", 0, 0, 1, "k")
            project_v("first", 0, "vx")
            for tile in range(T):
                max_scores("first", 0, 0, tile)
                if tile >= RING - 1:
                    keep_clock(2)
            keep_clock(7)
            max_row("first", 0, 0)
            keep_clock(3)
            for j in range(T):
                scores1("first", 0, 0, j)
                if j:
                    weigh(acc1, val, prob1, j - 1, s_p1, s_av1, 0)
            project_qk("first", 0, 1, 0, "q+")
            weigh(acc1, val, prob1, T - 1, s_p1, s_av1, 0)
            project_qk("first", 0, 1, 1, "k+")
            pe.wait_ge(s_wblk, 2)
            project_out("first", 0, 0)
            project_v("first", 0, "vx+")
            pe.wait_ge(s_es, 3)
            keep_clock(26)
            u_transposed(0)
            for k in range(RING):
                pe.wait_ge(*release(last_use(FIRST, k), "first", 0))

            with pe.Fori(0, B - 1) as i:
                for j in range(T):
                    scores2("body", i, i, j)
                    for tile in MX_AT[j]:
                        max_scores("body", i, i + 1, tile)
                    if j == 7:
                        max_row("body", i, i + 1)
                    if j:
                        weigh(acc2, u, prob2, j - 1, s_p2, s_av2, i)
                    if j == 6:
                        back_transposed("body", i, "yT-", y_flat, s_y, i + 1)
                scores1("body", i, i + 1, 0)
                weigh(acc2, u, prob2, T - 1, s_p2, s_av2, i)
                for j in range(1, T):
                    scores1("body", i, i + 1, j)
                    if j == 1:
                        att2_transposed(i)
                    if j == 7:
                        route("body", i, i)
                    weigh(acc1, val, prob1, j - 1, s_p1, s_av1, i + 1)
                    if j == 5:
                        w_transposed("body", i, i, WHOLE)
                project_qk("body", i, i + 2, 0, "q+")
                weigh(acc1, val, prob1, T - 1, s_p1, s_av1, i + 1)
                project_qk("body", i, i + 2, 1, "k+")
                project_out("body", i, i + 1)
                gates_transposed(i)
                experts("body", i, i, 0)
                experts("body", i, i, 1)
                expert_bias(i)
                project_v("body", i, "vx+")
                experts("body", i, i, 3)
                u_transposed(i + 1)
                experts("body", i, i, 2)

            b = B - 1
            for j in range(T):
                scores2("last", b, b, j)
                if j:
                    weigh(acc2, u, prob2, j - 1, s_p2, s_av2, b)
                if j == 6:
                    back_transposed("last", b, "yT-", y_flat, s_y, b + 1)
            weigh(acc2, u, prob2, T - 1, s_p2, s_av2, b)
            att2_transposed(b)
            keep_clock(28)
            w_transposed("last", b, b, HALVES)
            keep_clock(4)
            route("last", b, b)
            experts("last", b, b, 0)
            experts("last", b, b, 1)
            experts("last", b, b, 2)
            gates_transposed(b)
            experts("last", b, b, 3)
            pe.wait_ge(s_tk2, B)
            pe.wait_ge(s_gt, B)
            for t in SUM_ORDER:
                part_sum = (acc1, acc2)[t // 2][:, t % 2 * P:(t % 2 + 1) * P]
                pe.matmul(part_sum, tok2[:, 2 * t:2 * t + 2, :].rearrange("p h c -> p (h c)"), ident[:, :], start=True, stop=False)
                pe.matmul(part_sum, eb_blk[:, 2 * t:2 * t + 2, :].rearrange("p h c -> p (h c)"), gate_t[:, :],
                          start=False, stop=False)
                if t in ON_POOL or t == ON_VECTOR:
                    if t in ON_POOL:
                        pe.wait_ge(s_tail, ON_POOL.index(t) + 1)
                    else:
                        pe.wait_ge(s_tail_v, 1)
                    mm = pe.matmul(part_sum, ysum[:, 2 * t:2 * t + 2, :].rearrange("p h c -> p (h c)"), ident[:, :],
                                   start=False, stop=True)
                else:
                    pe.wait_ge(s_prod, (T // 2) * B + t + 1)
                    for e in range(E):
                        mm = pe.matmul(part_sum, prod[:, t, e].rearrange("p h c -> p (h c)"), ident[:, :],
                                       start=False, stop=(e == E - 1))
                mm.then_inc(s_yT, 1)

        @block.scalar
        def _(act):
            def filled(part, name, i):
                k, n, _ = place(part, name, i)
                act.wait_ge(s_fill, n + 1)
                return ring[:, k]

            def flat(buf):
                return buf.rearrange("p a n -> p (a n)")

            def round_x(slot):
                act.activation(xst[:, :], slot, ACT.Copy).then_inc(s_xr, 1)

            def round_q(part, i, name):
                act.activation(qst[0:ROW, :], flat(filled(part, name, i))[0:ROW, :], ACT.Copy).then_inc(s_qr, 1)

            def round_k(part, i, name):
                act.activation(kst[0:ROW, :], flat(filled(part, name, i))[0:ROW, :], ACT.Copy).then_inc(s_kr, 1)

            def keep_whole(part, i, name, rows, s):
                buf = filled(part, name, i)
                act.activation(qk_f[rows, :], flat(buf)[rows, :], ACT.Copy).then_inc(s, 1)

            def values(part, i, b, name):
                buf = filled(part, name, i)
                b4 = buf[:, :, 0:4 * (M + C)].rearrange("p a (t c) -> p a t c", c=M + C)
                act.activation(val[:, :, 0:M].rearrange("p (a t) c -> p a t c", a=2), b4[:, :, :, 0:M],
                               ACT.Copy).then_inc(s_vx, 1)
                act.wait_ge(s_tk1, b)
                act.activation(xt[:, :, :].rearrange("p (a t) c -> p a t c", a=2), b4[:, :, :, M:M + C],
                               ACT.Copy).then_inc(s_vx, 1)

            def max_row(part, i):
                buf = filled(part, "mrow", i)
                act.activation(kst[ROW:ROW + 2, 0:CHUNK], buf[ROW:ROW + 2, 0, :], ACT.Copy).then_inc(s_mrow, 1)

            def exp1(part, i, j):
                act.activation(prob1[:, j % 2, :], flat(filled(part, f"st{j}", i)), ACT.Exp).then_inc(s_p1, 1)

            def exp2(part, i, j):
                act.activation(prob2[:, j % 2, :], flat(filled(part, f"s{j}", i)), ACT.Exp, bias=shift[:, :],
                               accum_out=rsum2[:, j:j + 1]).then_inc(s_p2, 1)

            def copy_sums(dst, src, s_sum, b, s_ready):
                act.wait_ge(s_sum, b + 1)
                act.activation(dst, src, ACT.Copy).then_inc(s_ready, 1)

            def copy_high(b):
                act.wait_ge(s_un, b + 1)
                act.activation(uhl[:, :, 2, :], u[:, :, :], ACT.Copy).then_inc(s_uh, 1)

            def stack_swapped(b):
                act.wait_ge(s_uT, 2 * b + 2)
                act.activation(zsw[:, :], acc2[:, :].bitcast(F16), ACT.Copy).then_inc(s_z, 1)

            def round_w(part, i, b, pieces):
                k, used, _ = place(part, "wT" if part == "body" else "wT2", i)
                for n, piece in enumerate(pieces):
                    if n == len(pieces) - 1:
                        act.wait_ge(s_fill, used + 1)
                    else:
                        act.wait_ge(s_wT, n + 1)
                    act.activation(wst[:, columns(piece)], flat(ring[:, k])[:, columns(piece)], ACT.Copy).then_inc(s_wr, 1)

            def gap_exp(b):
                act.wait_ge(s_gap, b + 1)
                act.activation(gm[:, 3, :], gm[:, 2, :], ACT.Exp).then_inc(s_eg, 1)

            def copy_gates(b):
                act.wait_ge(s_gT, b + 1)
                act.activation(gate_t[:, :], acc2[0:T * E, 0:P], ACT.Copy).then_inc(s_gt, 1)

            def result(part, name, i, image):
                buf = filled(part, name, i)
                act.wait_ge(s_ob_free, image + 1)
                act.activation(ob[:, :], buf[:, 0, :], ACT.Copy).then_inc(s_ob, 1)

            act.wait_ge(s_x[0], 32)
            round_x(xin[:, 0, :])
            buf = filled("first", "w3", 0)
            for r in range(3):
                act.activation(w1[:, :, r, :], buf[:, 0, 0:2 * M].rearrange("p (a m) -> p a m", a=2), ACT.Copy).then_inc(s_wr1, 1)
            act.activation(vx1[:, 0:M], buf[:, 0, 2 * M:3 * M], ACT.Copy).then_inc(s_wr1, 1)
            round_q("first", 0, "q")
            round_k("first", 0, "k")
            values("first", 0, 0, "vx")
            act.wait_ge(s_x[1], 32)
            round_x(xin[:, 1, :])
            act.wait_ge(s_ew, (5 + T) * 16)
            act.activation(e1[:, :], e_in[:, :, :].rearrange("p e c -> p (e c)"), ACT.Copy).then_inc(s_er, 1)
            act.activation(r12[:, 0, :], r_in[:, :], ACT.Copy).then_inc(s_er, 1)
            max_row("first", 0)
            for j in range(T):
                exp1("first", 0, j)
            round_q("first", 0, "q+")
            copy_sums(agg[:, :], acc1[:, :], s_av1, 0, s_agg)
            keep_whole("first", 0, "q+", slice(M, 2 * M), s_qf)
            round_k("first", 0, "k+")
            keep_whole("first", 0, "k+", slice(2 * M, 3 * M), s_kf)
            values("first", 0, 1, "vx+")
            copy_high(0)
            stack_swapped(0)
            for b in range(2, B):
                act.wait_ge(s_x[b], 32)

            with act.Fori(0, B - 1) as i:
                for j in range(T - 1):
                    exp2("body", i, j)
                    if j == 4:
                        round_x(xin[:, bass.ds(i + 2, 1), :].rearrange("p a n -> p (a n)"))
                result("body", "yT-", i, i)
                exp2("body", i, T - 1)
                max_row("body", i)
                exp1("body", i, 0)
                copy_sums(att2[:, :], acc2[:, :], s_av2, i, s_att2)
                for j in range(1, T):
                    exp1("body", i, j)
                    if j == 5:
                        round_w("body", i, i, WHOLE)
                round_q("body", i, "q+")
                gap_exp(i)
                copy_sums(agg[:, :], acc1[:, :], s_av1, i + 1, s_agg)
                keep_whole("body", i, "q+", slice(M, 2 * M), s_qf)
                round_k("body", i, "k+")
                copy_gates(i)
                keep_whole("body", i, "k+", slice(2 * M, 3 * M), s_kf)
                values("body", i, i + 2, "vx+")
                copy_sums(ybias[:, :, :].rearrange("p t c -> p (t c)"), acc2[:, :], s_gb, i, s_gbs)
                copy_high(i + 1)
                stack_swapped(i + 1)

            b = B - 1
            for j in range(T):
                exp2("last", b, j)
                if j == 7:
                    result("last", "yT-", b, b)
            copy_sums(att2[:, :], acc2[:, :], s_av2, b, s_att2)
            round_w("last", b, b, HALVES)
            gap_exp(b)
            copy_gates(b)
            act.wait_ge(s_ob_free, B + 1)
            for half_sum in range(2):
                act.wait_ge(s_yT, 2 * (half_sum + 1))
                cols = slice(half_sum * CHUNK // 2, (half_sum + 1) * CHUNK // 2)
                act.activation(ob[:, cols], (acc1, acc2)[half_sum][:, 0:CHUNK // 2], ACT.Copy).then_inc(s_ob, 1)

        @block.vector
        def _(dve):
            def filled(part, name, i):
                k, n, _ = place(part, name, i)
                dve.wait_ge(s_fill, n + 1)
                return ring[:, k]

            def flat(buf):
                return buf.rearrange("p a n -> p (a n)")

            def wide(a, n):
                return a.unsqueeze(2).to_broadcast([P, T, n])

            def split_x(b, slot):
                dve.wait_ge(s_xr, b + 1)
                lo = xst[C:P, :]
                dve.tensor_tensor(lo, slot, lo.bitcast(F32), ALU.subtract).then_inc(s_xs, 1)

            def split_q(part, i, b):
                buf = filled(part, "q", i)
                dve.wait_ge(s_qr, b + 1)
                lo = qst[M:2 * M, :]
                dve.tensor_tensor(lo, flat(buf)[M:2 * M, :], lo.bitcast(F32), ALU.subtract).then_inc(s_qks, 1)

            def split_k(part, i, b):
                buf = filled(part, "k", i)
                dve.wait_ge(s_kr, b + 1)
                lo = kst[2 * M:3 * M, :]
                dve.tensor_tensor(lo, flat(buf)[2 * M:3 * M, :], lo.bitcast(F32), ALU.subtract).then_inc(s_qks, 1)

            def row_max(part, i, tile):
                dve.tensor_reduce(rowmax[:, tile:tile + 1], flat(filled(part, f"mx{tile}", i)), AX.X, ALU.max).then_inc(s_mx, 1)

            def negate_max(b):
                dve.wait_ge(s_mx, T * (b + 1))
                hi = nmax[:, :, ROW:ROW + 1]
                rm = rowmax[:, :].unsqueeze(2)
                dve.tensor_scalar(hi, rm, -1.0, None, ALU.mult).then_inc(s_nm, 1)
                dve.wait_ge(s_nm, 2 * b + 1)
                dve.scalar_tensor_tensor(out=nmax[:, :, ROW + 1:ROW + 2], in0=rm, scalar=-1.0, in1=hi.bitcast(F32),
                                         op0=ALU.mult, op1=ALU.subtract).then_inc(s_nm, 1)

            def max_row(part, i):
                buf = filled(part, "mrow", i)
                dve.tensor_copy(kst[ROW:ROW + 2, CHUNK:N], buf[ROW:ROW + 2, 1, :]).then_inc(s_mrow, 1)

            def tokens1(part, i, b):
                buf = filled(part, "po", i)
                po = buf[:, :, 0:4 * (C + 1)].rearrange("p a (t c) -> p a t c", c=C + 1)
                r4 = rinv1[:, :].rearrange("p (a t) -> p a t", a=2).unsqueeze(3)
                dve.reciprocal(r4, po[:, :, :, C:C + 1]).then_inc(s_t1, 1)
                dve.wait_ge(s_t1, b + 1)
                dve.tensor_tensor(tdiv[:, :, :].rearrange("p (a t) c -> p a t c", a=2), po[:, :, :, 0:C],
                                  r4.to_broadcast([P, 2, 4, C]), ALU.mult).then_inc(s_po, 1)
                dve.wait_ge(s_po, b + 1)
                dve.wait_ge(s_vx, 2 * b + 2)
                dve.tensor_tensor(tok1[:, :, :], tdiv[:, :, :], xt[:, :, :], ALU.add).then_inc(s_tk1, 1)

            def norm_stats(tok, s_tok, stats, sm, cen, s_ln, s_ve, s_cen, b):
                dve.wait_ge(s_tok, b + 1)
                ln = Steps(dve, s_ln, 3, b)
                for tile in range(T):
                    last = dve.bn_stats(stats[:, tile, :], tok[:, tile, :])
                ln.then(last)
                mean_e, var_e, mean_o, var_o = (stats[:, :, k] for k in (1, 2, 4, 5))
                dve.tensor_tensor(sm[:, 0, :], mean_e, mean_o, ALU.subtract)
                dve.scalar_tensor_tensor(out=sm[:, 4, :], in0=var_e, scalar=C * EPS, in1=var_o, op0=ALU.add, op1=ALU.add)
                ln.then(dve.tensor_tensor(sm[:, 1, :], mean_e, mean_o, ALU.add))
                dve.scalar_tensor_tensor(out=sm[:, 5, :], in0=sm[:, 0, :], scalar=C / 4.0, in1=sm[:, 0, :],
                                         op0=ALU.mult, op1=ALU.mult)
                ln.then(dve.tensor_scalar(sm[:, 6, :], sm[:, 1, :], -ROOT_C / 2, None, ALU.mult))
                ln.end()
                dve.tensor_tensor(sm[:, 2, :], sm[:, 4, :], sm[:, 5, :], ALU.add).then_inc(s_ve, 1)
                dve.scalar_tensor_tensor(out=cen[:, :, :], in0=tok[:, :, :], scalar=ROOT_C, in1=wide(sm[:, 6, :], C),
                                         op0=ALU.mult, op1=ALU.add).then_inc(s_cen, 1)

            def normalize1(b):
                dve.wait_ge(s_cen1, b + 1)
                dve.wait_ge(s_rs1, b + 1)
                dve.tensor_tensor(u[:, :, :], cen1[:, :, :], wide(sm1[:, 3, :], C), ALU.mult).then_inc(s_un, 1)
                dve.wait_ge(s_un, b + 1)
                dve.tensor_copy(uhl[:, :, 0, :], u[:, :, :]).then_inc(s_uh1, 1)
                dve.wait_ge(s_uh1, b + 1)
                dve.tensor_tensor(uhl[:, :, 1, :], u[:, :, :], uhl[:, :, 0, :], ALU.subtract).then_inc(s_u, 1)

            def stack_u(b):
                dve.wait_ge(s_uT, 2 * b + 1)
                dve.tensor_copy(zst[:, :], acc1[:, :].bitcast(F16)).then_inc(s_z, 1)

            def tokens2(b):
                dve.wait_ge(s_p2, T * (b + 1))
                dve.reciprocal(rinv2[:, :], rsum2[:, :]).then_inc(s_t2, 1)
                dve.wait_ge(s_t2, b + 1)
                dve.wait_ge(s_o, b + 1)
                dve.tensor_tensor(odiv[:, :, :], acc2[:, :].rearrange("p (t c) -> p t c", c=C), wide(rinv2[:, :], C),
                                  ALU.mult).then_inc(s_oT, 1)
                dve.wait_ge(s_oT, b + 1)
                dve.tensor_tensor(tok2[:, :, :], odiv[:, :, :], tok1[:, :, :], ALU.add).then_inc(s_tk2, 1)

            def normalize2(b, pieces):
                dve.wait_ge(s_cen2, b + 1)
                dve.wait_ge(s_rs2, b + 1)
                for piece in pieces:
                    step = 3 - piece.stop + piece.start
                    tiles = slice(piece.start, T, step) if step == 2 else slice(0, T)
                    shape = [P, T // step, 2, C]
                    dve.tensor_tensor(wdup[:, tiles, :, :], cen2[:, tiles, :].unsqueeze(2).to_broadcast(shape),
                                      sm2[:, 3, tiles].unsqueeze(2).unsqueeze(3).to_broadcast(shape), ALU.mult).then_inc(s_w, 1)

            def split_w(part, i, b, pieces):
                k, _, _ = place(part, "wT" if part == "body" else "wT2", i)
                for n, piece in enumerate(pieces):
                    dve.wait_ge(s_wr, b + n + 1)
                    lo = wst[C:P, columns(piece)]
                    dve.tensor_tensor(lo, flat(ring[:, k])[C:P, columns(piece)], lo.bitcast(F32), ALU.subtract).then_inc(s_ws, 1)

            def top2(part, i, b):
                buf = filled(part, "rt", i)
                parts = buf[:, 0, 0:2 * T * E].rearrange("p (t a e) -> p t a e", a=2, e=E)
                dve.tensor_tensor(lg_1[:, :, :], parts[:, :, 0, :],
                                  rb_all[:, :].unsqueeze(1).to_broadcast([P, T, E]), ALU.add).then_inc(s_lg1, 1)
                dve.wait_ge(s_lg1, b + 1)
                dve.tensor_tensor(lg[:, :, :], parts[:, :, 1, :], lg_1[:, :, :], ALU.add).then_inc(s_lg, 1)
                dve.wait_ge(s_lg, b + 1)
                top = Steps(dve, s_top, 9, b)
                dve.tensor_copy(landing[:, :], lg[:, 0, 0:1])
                for tile in range(T):
                    last = dve.max(top8[:, tile, :], lg[:, tile, :])
                top.then(last)
                dve.tensor_tensor(gm[:, 2, :], top8[:, :, 1], top8[:, :, 0], ALU.subtract).then_inc(s_gap, 1)
                both = lg[:, :, :].unsqueeze(1).to_broadcast([P, 2, T, E])
                top.then(dve.tensor_tensor(cand[:, :, :, :], both, top8[:, :, 0:2].rearrange("p t n -> p n t").unsqueeze(3)
                                           .to_broadcast([P, 2, T, E]), ALU.is_equal))
                top.then(dve.tensor_tensor(cand[:, :, :, :], cand[:, :, :, :],
                                           ramp[:, :, :].unsqueeze(1).to_broadcast([P, 2, T, E]), ALU.mult))
                top.then(dve.tensor_reduce(gm[:, 0, :], cand[:, 0, :, :], AX.X, ALU.max))
                top.then(dve.tensor_tensor(pick1[:, :, :], cand[:, 0, :, :], wide(gm[:, 0, :], E), ALU.is_equal))
                dve.scalar_tensor_tensor(out=cand2[:, :, :], in0=pick1[:, :, :], scalar=-2.0 * E, in1=cand[:, 1, :, :],
                                         op0=ALU.mult, op1=ALU.add)
                dve.wait_ge(s_eg, b + 1)
                top.then(dve.tensor_scalar(gm[:, 4, :], gm[:, 3, :], 1.0, None, ALU.add))
                dve.tensor_reduce(gm[:, 1, :], cand2[:, :, :], AX.X, ALU.max)
                top.then(dve.reciprocal(gm[:, 5, :], gm[:, 4, :]))
                dve.tensor_tensor(pick2[:, :, :], cand2[:, :, :], wide(gm[:, 1, :], E), ALU.is_equal)
                top.then(dve.tensor_tensor(gm[:, 6, :], gm[:, 3, :], gm[:, 5, :], ALU.mult))
                dve.tensor_tensor(pick2[:, :, :], pick2[:, :, :], wide(gm[:, 6, :], E), ALU.mult)
                top.then(dve.tensor_tensor(pick1[:, :, :], pick1[:, :, :], wide(gm[:, 5, :], E), ALU.mult))
                top.end()
                dve.tensor_tensor(gate[:, 0:T, :], pick1[:, :, :], pick2[:, :, :], ALU.add).then_inc(s_gate, 1)

            def weigh_experts(part, i, b, g):
                buf = filled(part, f"e{g}", i)
                if g == 0:
                    dve.wait_ge(s_gate, b + 1)
                dve.wait_ge(s_half, (T // 2) * b + g + 1)
                gates = gate[:, 2 * g:2 * g + 2, :].unsqueeze(3).to_broadcast([P, 2, E, C])
                dve.tensor_tensor(prod[:, g].rearrange("p e h c -> p h e c"), buf.rearrange("p h (e c) -> p h e c", c=C),
                                  gates, ALU.mult).then_inc(s_prod, 1)

            dve.memset(filler[:, :], 1.0).then_inc(s_filler, 1)
            dve.wait_ge(s_const, 2)
            dve.tensor_copy(ident_r[:, :], ident[:, :])
            dve.tensor_tensor(vx1[:, M:M + C], ident[:, 0:C], ident[:, C:P], ALU.add).then_inc(s_wts, 1)
            dve.memset(qst[ROW:ROW + 2, :].bitcast(F32), 1.0)
            dve.memset(shift[:, :], -SHIFT).then_inc(s_shift, 1)
            split_x(0, xin[C:P, 0, :])
            buf = filled("first", "w3", 0)
            dve.wait_ge(s_wr1, 4)
            dve.tensor_tensor(w2[:, :, :, :], buf[:, 0, 0:2 * M].rearrange("p (a m) -> p a m", a=2).unsqueeze(2)
                              .to_broadcast([P, 2, 3, M]), w1[:, :, :, :].bitcast(F32), ALU.subtract).then_inc(s_wts, 1)
            dve.memset(vx2[:, M:M + C].bitcast(F32), 0.0)
            dve.tensor_tensor(vx2[:, 0:M], buf[:, 0, 2 * M:3 * M], vx1[:, 0:M].bitcast(F32), ALU.subtract).then_inc(s_wts, 1)
            buf = filled("first", "wo", 0)
            dve.wait_ge(s_const, 4)
            for h in range(2):
                dve.memset(wo_blk[h * C + ONE:h * C + ONE + 1, h, C:C + 1], 1.0)
                dve.tensor_copy(wo_blk[h * C:(h + 1) * C, h, 0:C], buf[h * C:(h + 1) * C, 0, 0:C]).then_inc(s_wblk, 1)
            dve.tensor_copy(ident_h[:, :], ident[:, :])
            split_q("first", 0, 0)
            split_k("first", 0, 0)
            for tile in range(T):
                row_max("first", 0, tile)
            negate_max(0)
            max_row("first", 0)
            dve.wait_ge(s_er, 2)
            dve.tensor_tensor(e2[:, :], e_in[:, :, :].rearrange("p e c -> p (e c)"), e1[:, :].bitcast(F32),
                              ALU.subtract).then_inc(s_es, 1)
            dve.tensor_tensor(r12[:, 1, :], r_in[:, :], r12[:, 0, :].bitcast(F32), ALU.subtract).then_inc(s_es, 1)
            dve.wait_ge(s_const, 5)
            dve.tensor_tensor(eb_blk[:, :, :], eb_in[:, :].unsqueeze(1).to_broadcast([T * E, T, C]),
                              tile_mask[:, :].unsqueeze(2).to_broadcast([T * E, T, C]), ALU.mult).then_inc(s_es, 1)
            tokens1("first", 0, 0)
            norm_stats(tok1, s_tk1, stats1, sm1, cen1, s_ln1, s_ve1, s_cen1, 0)
            normalize1(0)
            stack_u(0)

            with dve.Fori(0, B - 1) as i:
                for tile in range(T):
                    row_max("body", i, tile)
                negate_max(i + 1)
                max_row("body", i)
                tokens2(i)
                norm_stats(tok2, s_tk2, stats2, sm2, cen2, s_ln2, s_ve2, s_cen2, i)
                normalize2(i, WHOLE)
                split_w("body", i, i, WHOLE)
                top2("body", i, i)
                tokens1("body", i, i + 1)
                norm_stats(tok1, s_tk1, stats1, sm1, cen1, s_ln1, s_ve1, s_cen1, i + 1)
                weigh_experts("body", i, i, 0)
                normalize1(i + 1)
                weigh_experts("body", i, i, 1)
                stack_u(i + 1)
                weigh_experts("body", i, i, 2)
                weigh_experts("body", i, i, 3)

            b = B - 1
            tokens2(b)
            norm_stats(tok2, s_tk2, stats2, sm2, cen2, s_ln2, s_ve2, s_cen2, b)
            normalize2(b, HALVES)
            split_w("last", b, b, HALVES)
            top2("last", b, b)
            for g in range(T // 2):
                weigh_experts("last", b, b, g)
            t = ON_VECTOR
            dve.wait_ge(s_prod, (T // 2) * B + t + 1)
            dve.tensor_reduce(ysum[:, 2 * t:2 * t + 2, :], prod[:, t].rearrange("p e h c -> p h c e"), AX.X,
                              ALU.add).then_inc(s_tail_v, 1)


_INS = ["x", "L0_conv_wq", "L0_conv_wk", "L0_conv_wv", "L0_conv_wo", "L1_ffn_router_w", "L1_ffn_router_b",
        "L1_ffn_expert_w", "L1_ffn_expert_b"]


def kernel(**inputs):
    import numpy as _np
    import concourse.bacc as _bacc
    from concourse import mybir as _mybir
    from concourse.bass_utils import run_bass_kernel_spmd as _run

    nc = _bacc.Bacc("TRN2", target_bir_lowering=False, num_devices=1)
    arrays, args = {}, []
    for name in _INS:
        a = _np.ascontiguousarray(inputs[name])
        arrays[f"in_{name}"] = a
        args.append(nc.dram_tensor(f"in_{name}", a.shape, _mybir.dt.from_np(a.dtype), kind="ExternalInput").ap())
    shape = inputs["x"].shape
    args.append(nc.dram_tensor("out_0", shape, _mybir.dt.float32, kind="ExternalOutput").ap())
    build(nc, *args)
    return _run(nc, [arrays], core_ids=[0]).results[0]["out_0"]
```

```python
from contextlib import ExitStack

import concourse.bass as bass
from concourse import mybir

ALU = mybir.AluOpType
ACT = mybir.ActivationFunctionType
AX = mybir.AxisListType
F32 = mybir.dt.float32
F32R = mybir.dt.float32r
F16 = mybir.dt.float16

P = 128
B, C, N, M, E = 4, 64, 1024, 32, 8
CHUNK = 512
T = N // P
EPS = 1e-5
ONE = M
ROW = 3 * M
ROOT_C = float(C) ** 0.5
SHIFT = float(C) / 2

RING = 3
ON_POOL = [0, 2]
ON_VECTOR = 3
SUM_ORDER = [1, 0, 3, 2]
MX_AT = [[], [0], [1, 2], [3], [4, 5], [6, 7], [], []]
FIRST = (["w3", "q", "k", "vx"] + [f"mx{i}" for i in range(T)] + ["mrow"] + [f"st{j}" for j in range(T)]
         + ["q+", "k+", "po", "vx+"])
BODY = []
LAST = []
for j in range(T):
    BODY += ["mrow"] * (j == 7) + [f"s{j}"] + [f"mx{i}" for i in MX_AT[j]] + ["yT-"] * (j == 5)
    LAST += [f"s{j}"]
for j in range(T):
    BODY += [f"st{j}"] + {5: ["wT"], 7: ["rt"]}.get(j, [])
BODY = [(name, n % RING) for n, name in enumerate(BODY)]
BODY += [("q+", 1), ("k+", 2), ("po", 0), ("e0", 1), ("e1", 0), ("vx+", 2), ("e3", 2), ("e2", 1)]
LAST += ["yT-", "wT", "rt", "e0", "e1", "e2", "e3"]
LAST = [(name, n % RING) for n, name in enumerate(LAST)]
FIRST = [(name, n % RING) for n, name in enumerate(FIRST)]


def chunk(h):
    return slice(h * CHUNK, (h + 1) * CHUNK)


def use(uses, name):
    return [n for n, _ in uses].index(name)


def last_use(uses, buf):
    return ([n for n, b in uses if b == buf] or [None])[-1]


def col(tile):
    return (tile % 2) * CHUNK + (tile // 2) * P


def build(nc, x, wq, wk, wv, wo, rw, rb, ew, eb, out):
    ctx = ExitStack()
    with ctx:
        def sb(name, shape, dt=F32):
            return ctx.enter_context(nc.sbuf_tensor(name, shape, dt))

        def sem(name):
            return ctx.enter_context(nc.semaphore(name))

        ident = sb("ident", [P, P])
        ident_h = sb("ident_h", [P, P], F16)
        ident_r = sb("ident_r", [P, P], F32R)
        filler = sb("filler", [P, CHUNK], F16)
        minus_half = sb("minus_half", [P, T])
        shift = sb("shift", [P, 1])
        ramp = sb("ramp", [P, T, E])
        w3 = sb("w3", [ROW, 2, C])
        wo4 = sb("wo4", [C, 4, M])
        w1 = sb("w1", [P, 2, 3, M], F32R)
        w2 = sb("w2", [P, 2, 3, M], F32R)
        vx1 = sb("vx1", [P, M + C], F32R)
        vx2 = sb("vx2", [P, M + C], F32R)
        wo_blk = sb("wo_blk", [P, 2, C + 1])
        e_in = sb("e_in", [P, E, C])
        e1 = sb("e1", [P, E * C], F32R)
        e2 = sb("e2", [P, E * C], F32R)
        r_in = sb("r_in", [P, E])
        r12 = sb("r12", [P, 2, E], F32R)
        rb_all = sb("rb_all", [P, E])
        eb_in = sb("eb_in", [T * E, C])
        eb_blk = sb("eb_blk", [T * E, T, C])
        tile_mask = sb("tile_mask", [T * E, T])

        xin = sb("xin", [P, B + 1, N])
        xst = sb("xst", [P, N], F32R)
        qst = sb("qst", [P, N], F32R)
        kst = sb("kst", [P, N], F32R)
        qk_f = sb("qk_f", [P, N])
        val = sb("val", [P, T, C])
        xt = sb("xt", [P, T, C])
        rowmax = sb("rowmax", [P, T])
        nmax = sb("nmax", [P, T, ROW + 2], F32R)
        prob1 = sb("prob1", [P, 2, N])
        prob2 = sb("prob2", [P, 2, N])
        agg = sb("agg", [P, CHUNK])
        rinv1 = sb("rinv1", [P, T])
        tok1 = sb("tok1", [P, T, C])
        tdiv = sb("tdiv", [P, T, C])
        stats1 = sb("stats1", [P, T, 6])
        sm1 = sb("sm1", [P, 7, T])
        cen1 = sb("cen1", [P, T, C])
        u = sb("u", [P, T, C])
        uhl = sb("uhl", [P, T, 3, C], F16)
        zst = sb("zst", [P, N], F16)
        zsw = sb("zsw", [P, N], F16)
        rsum2 = sb("rsum2", [P, T])
        rinv2 = sb("rinv2", [P, T])
        att2 = sb("att2", [P, CHUNK])
        tok2 = sb("tok2", [P, T, C])
        odiv = sb("odiv", [P, T, C])
        stats2 = sb("stats2", [P, T, 6])
        sm2 = sb("sm2", [P, 7, T])
        cen2 = sb("cen2", [P, T, C])
        wdup = sb("wdup", [P, T, 2, C])
        wst = sb("wst", [P, N], F32R)
        lg_1 = sb("lg_1", [P, T, E])
        lg = sb("lg", [P, T, E])
        top8 = sb("top8", [P, T, E])
        cand = sb("cand", [P, 2, T, E])
        cand2 = sb("cand2", [P, T, E])
        landing = sb("landing", [P, 1])
        pick1 = sb("pick1", [P, T, E])
        pick2 = sb("pick2", [P, T, E])
        gm = sb("gm", [P, 7, T])
        gate = sb("gate", [P, 2 * T, E])
        gate_t = sb("gate_t", [T * E, P])
        prod = sb("prod", [P, T // 2, E, 2, C])
        half = sb("half", [P, E // 2, 2, C])
        quart = sb("quart", [P, E // 4, 2, C])
        ysum = sb("ysum", [P, T, C])
        ybias = sb("ybias", [P, T, C])
        yres = sb("yres", [P, T, C])
        y = sb("y", [P, T, C])
        ob = sb("ob", [P, CHUNK])

        ring = ctx.enter_context(nc.psum_tensor("ring", [P, RING, 2, CHUNK], F32))
        acc1 = ctx.enter_context(nc.psum_tensor("acc1", [P, CHUNK], F32))
        acc2 = ctx.enter_context(nc.psum_tensor("acc2", [P, CHUNK], F32))

        s_fill = sem("ring_filled")
        s_const = sem("const_ready")
        s_filler = sem("filler_ready")
        s_pool = sem("pool_step")
        s_shift = sem("shift_ready")
        s_w3 = sem("w3_loaded")
        s_wol = sem("wo_loaded")
        s_ew = sem("experts_loaded")
        s_x = [sem(f"x_loaded{b}") for b in range(B)]
        s_wr1 = sem("weights_rounded")
        s_wts = sem("weights_split")
        s_woT = sem("wo_turned")
        s_wblk = sem("wo_blk_ready")
        s_er = sem("experts_rounded")
        s_es = sem("experts_split")
        s_xr = sem("x_rounded")
        s_xs = sem("x_split")
        s_qr = sem("q_rounded")
        s_kr = sem("k_rounded")
        s_qk0 = sem("chunk_projected")
        s_qf = sem("q_copied")
        s_kf = sem("k_copied")
        s_qks = sem("qk_split")
        s_vx = sem("v_and_x_ready")
        s_mx = sem("rowmax_ready")
        s_nm = sem("negmax_split")
        s_mrow = sem("maxrow_ready")
        s_p1 = sem("probs1_ready")
        s_av1 = sem("agg_summed")
        s_agg = sem("agg_ready")
        s_po = sem("projection_read")
        s_t1 = sem("tok1_step")
        s_tk1 = sem("tok1_ready")
        s_ln1 = sem("ln1_step")
        s_ve1 = sem("var1_ready")
        s_cen1 = sem("centered1_ready")
        s_rs1 = sem("rstd1_ready")
        s_un = sem("u_step")
        s_uh1 = sem("u_high_ready")
        s_uh = sem("u_high_copied")
        s_u = sem("uhl_ready")
        s_uT = sem("u_transposed")
        s_z = sem("z_ready")
        s_p2 = sem("probs2_ready")
        s_av2 = sem("att2_summed")
        s_att2 = sem("att2_ready")
        s_o = sem("att2_turned")
        s_oT = sem("att2_read")
        s_t2 = sem("rinv2_ready")
        s_tk2 = sem("tok2_ready")
        s_ln2 = sem("ln2_step")
        s_ve2 = sem("var2_ready")
        s_cen2 = sem("centered2_ready")
        s_rs2 = sem("rstd2_ready")
        s_wT = sem("w_transposed")
        s_w = sem("w_ready")
        s_wr = sem("w_rounded")
        s_ws = sem("w_split")
        s_lg1 = sem("logits_first_part")
        s_lg = sem("logits_ready")
        s_top = sem("top2_step")
        s_gap = sem("logit_gap_ready")
        s_eg = sem("gap_exp_ready")
        s_gate = sem("gates_ready")
        s_gT = sem("gates_turned")
        s_gt = sem("gates_transposed")
        s_gb = sem("expert_bias_summed")
        s_gbs = sem("ybias_ready")
        s_prod = sem("prods_ready")
        s_half = sem("prods_used")
        s_tree = sem("tree_step")
        s_tail = sem("last_experts_summed")
        s_tail_v = sem("last_experts_summed_v")
        s_yT = sem("last_y_turned")
        s_y = sem("y_ready")
        s_ob = sem("out_ready")
        s_out = sem("out_stored")
        s_ob_free = sem("ob_free")

        RELEASE = {"w3": (s_wts, 3, 3), "q": (s_qks, 2, 2), "k": (s_qks, 2, 4), "vx": (s_vx, 2, 2),
                   "q+": (s_qf, 1, 1), "k+": (s_kf, 1, 1), "vx+": (s_vx, 2, 4),
                   "mrow": (s_mrow, 2, 2), "po": (s_po, 1, 1),
                   "wT": (s_ws, 2, 2), "rt": (s_lg, 1, 1), "yT-": (s_ob, 1, 2)}
        RELEASE.update({f"mx{i}": (s_mx, T, i + 1) for i in range(T)})
        RELEASE.update({f"st{j}": (s_p1, T, j + 1) for j in range(T)})
        RELEASE.update({f"s{j}": (s_p2, T, j + 1) for j in range(T)})
        RELEASE.update({f"e{g}": (s_prod, T // 2, T // 2 + g + 1) for g in range(T // 2)})
        NEXT = {"q+", "k+", "vx+", "mrow", "po"} | {f"mx{i}" for i in range(T)} | {f"st{j}" for j in range(T)}

        def release(name, part, i):
            s, per, at = RELEASE[name]
            image = i + (part == "body" and name in NEXT) - (name == "yT-")
            return s, image * per + at

        def place(part, name, i):
            uses = {"first": FIRST, "body": BODY, "last": LAST}[part]
            idx = use(uses, name)
            k = uses[idx][1]
            before = last_use(uses[:idx], k)
            if part == "first":
                return k, idx, (before, "first", 0) if before else None
            if part == "body":
                before = (before, "body", i) if before else (last_use(BODY, k), "body", i - 1)
                return k, len(FIRST) + i * len(BODY) + idx, before
            before = (before, "last", B - 1) if before else (last_use(BODY, k), "body", B - 2)
            return k, len(FIRST) + (B - 1) * len(BODY) + idx, before

        class Steps:

            def __init__(self, engine, s, per_image, b):
                self.engine, self.s, self.per, self.base, self.n = engine, s, per_image, b * per_image, 0

            def then(self, instruction):
                self.n += 1
                instruction.then_inc(self.s, 1)
                self.engine.wait_ge(self.s, self.base + self.n)

            def end(self):
                assert self.n == self.per, (self.n, self.per)

        block = ctx.enter_context(nc.Block())

        @block.sync
        def _(sp):
            def load_x(b):
                for h in range(2):
                    sp.dma_start(xin[h * C:(h + 1) * C, b, :], x[b].rearrange("c h w -> c (h w)")).then_inc(s_x[b], 16)

            load_x(0)
            for n, w in enumerate((wq, wk, wv)):
                sp.dma_start(w3[n * M:(n + 1) * M, :, :], w.unsqueeze(1).to_broadcast([M, 2, C])).then_inc(s_w3, 16)
            sp.wait_ge(s_const, 1)
            for h in range(2):
                sp.dma_start(wo4[:, 2 * h, :], wo).then_inc(s_wol, 16)
            load_x(1)
            for h in range(2):
                sp.dma_start(e_in[h * C:(h + 1) * C, :, :], ew.rearrange("e d c -> d e c")).then_inc(s_ew, 16)
                sp.dma_start(r_in[h * C:(h + 1) * C, :], rw).then_inc(s_ew, 16)
            sp.dma_start(rb_all[:, :], rb.rearrange("(a e) -> a e", a=1).to_broadcast([P, E])).then_inc(s_ew, 16)
            for t in range(T):
                sp.dma_start(eb_in[t * E:(t + 1) * E, :], eb).then_inc(s_ew, 16)
            for b in range(2, B):
                load_x(b)

            def store(b, image):
                sp.wait_ge(s_ob, b + 2)
                for h in range(2):
                    sp.dma_start(image[:, chunk(h)], ob[h * C:(h + 1) * C, :]).then_inc(s_out, 16)
                sp.wait_ge(s_out, 2 * 16 * (b + 1))
                sp.sem_inc(s_ob_free, 1)

            flat = out.rearrange("b c h w -> (b c) (h w)")
            sp.sem_inc(s_ob_free, 2)
            with sp.Fori(0, B - 1) as i:
                store(i, flat[bass.ds(i * C, C), :])
            for half_sum in range(2):
                sp.wait_ge(s_ob, B + 1 + half_sum)
                lo, hi = half_sum * CHUNK // 2, (half_sum + 1) * CHUNK // 2
                for h in range(2):
                    sp.dma_start(flat[(B - 1) * C:B * C, h * CHUNK + lo:h * CHUNK + hi],
                                 ob[h * C:(h + 1) * C, lo:hi]).then_inc(s_out, 16)
            sp.wait_ge(s_out, 2 * 16 * (B + 1))

        @block.gpsimd
        def _(pool):
            pool.memset(wo4[:, :, :], 0.0).then_inc(s_const, 1)
            pool.memset(ident[:, :], 0.0).then_inc(s_pool, 1)
            pool.wait_ge(s_pool, 1)
            pool.affine_select(out=ident[:, :], in_=ident[:, :], compare_op=ALU.not_equal, fill=1.0, base=0,
                               pattern=[[-1, P]], channel_multiplier=1).then_inc(s_const, 1)
            pool.memset(nmax[:, :, :].bitcast(F32), 0.0)
            pool.memset(val[:, :, M + 1:C], 0.0)
            pool.memset(val[:, :, ONE:ONE + 1], 1.0).then_inc(s_const, 1)
            pool.memset(wo_blk[:, :, :], 0.0).then_inc(s_const, 1)
            pool.memset(minus_half[:, :], -0.5).then_inc(s_half, T // 2)
            pool.memset(y[:, :, :], 0.0).then_inc(s_y, 1)
            pool.memset(gate[:, T:2 * T, :], 0.0).then_inc(s_gbs, 1)
            pool.memset(xin[:, B, :], 0.0).then_inc(s_prod, T // 2)
            for e in range(E):
                last = pool.memset(ramp[:, :, e:e + 1], float(E - e))
            pool.memset(tile_mask[:, :], 1.0).then_inc(s_pool, 1)
            pool.wait_ge(s_pool, 2)
            pool.affine_select(out=tile_mask[:, :], in_=tile_mask[:, :], compare_op=ALU.is_ge, fill=0.0, base=0,
                               pattern=[[-E, T]], channel_multiplier=1).then_inc(s_pool, 1)
            pool.wait_ge(s_pool, 3)
            pool.affine_select(out=tile_mask[:, :], in_=tile_mask[:, :], compare_op=ALU.is_ge, fill=0.0, base=E - 1,
                               pattern=[[E, T]], channel_multiplier=-1).then_inc(s_const, 1)

            def rstd(b, s_ve, s_rs, sm):
                pool.wait_ge(s_ve, b + 1)
                pool.tensor_tensor(sm[:, 3, :], sm[:, 2, :], minus_half[:, :], ALU.pow).then_inc(s_rs, 1)

            def split_x(b, slot):
                pool.wait_ge(s_xr, b + 2)
                first = xst[C:P, :]
                pool.tensor_tensor(first, slot, first.bitcast(F32), ALU.subtract).then_inc(s_xs, 1)
                pool.wait_ge(s_xs, b + 2)

            def split_q(b):
                pool.wait_ge(s_qf, b)
                first = qst[M:2 * M, :]
                pool.tensor_tensor(first, qk_f[M:2 * M, :], first.bitcast(F32), ALU.subtract).then_inc(s_qks, 1)
                pool.wait_ge(s_qks, 2 * b + 3)

            def split_k(b):
                pool.wait_ge(s_kf, b)
                first = kst[2 * M:3 * M, :]
                pool.tensor_tensor(first, qk_f[2 * M:3 * M, :], first.bitcast(F32), ALU.subtract).then_inc(s_qks, 1)
                pool.wait_ge(s_qks, 2 * b + 4)

            def sum_pair(b, g, tree):
                pool.wait_ge(s_prod, (T // 2) * (b + 1) + g + 1)
                p = prod[:, g]
                pool.tensor_tensor(half[:, :, :, :], p[:, 0:E // 2], p[:, E // 2:E], ALU.add).then_inc(s_half, 1)
                pool.wait_ge(s_half, (T // 2) * (b + 1) + g + 1)
                tree.then(pool.tensor_tensor(quart[:, :, :, :], half[:, 0:E // 4], half[:, E // 4:E // 2], ALU.add))
                tree.then(pool.tensor_tensor(ysum[:, 2 * g:2 * g + 2, :], quart[:, 0], quart[:, 1], ALU.add))

            def residual(b, tree):
                tree.then(pool.tensor_tensor(yres[:, :, :], ysum[:, :, :], tok2[:, :, :], ALU.add))
                pool.wait_ge(s_gbs, b + 2)
                pool.tensor_tensor(y[:, :, :], yres[:, :, :], ybias[:, :, :], ALU.add).then_inc(s_y, 1)

            pool.wait_ge(s_const, 5)
            split_x(1, xin[C:P, 1, :])
            split_q(1)
            rstd(0, s_ve1, s_rs1, sm1)
            pool.wait_ge(s_rs1, 1)
            split_k(1)
            with pool.Fori(0, B - 1) as i:
                pool.wait_ge(s_y, i + 1)
                split_x(i + 2, xin[C:P, bass.ds(i + 2, 1), :].rearrange("p a n -> p (a n)"))
                rstd(i, s_ve2, s_rs2, sm2)
                pool.wait_ge(s_rs2, i + 1)
                split_q(i + 2)
                rstd(i + 1, s_ve1, s_rs1, sm1)
                pool.wait_ge(s_rs1, i + 2)
                split_k(i + 2)
                tree = Steps(pool, s_tree, 2 * (T // 2) + 1, i)
                for g in range(T // 2):
                    sum_pair(i, g, tree)
                residual(i, tree)
                tree.end()
            b = B - 1
            rstd(b, s_ve2, s_rs2, sm2)
            for n, g in enumerate(ON_POOL):
                pool.wait_ge(s_prod, (T // 2) * (b + 1) + g + 1)
                pool.tensor_tensor(half[:, :, :, :], prod[:, g, 0:E // 2], prod[:, g, E // 2:E], ALU.add).then_inc(s_half, 1)
                pool.wait_ge(s_half, (T // 2) * (b + 1) + n + 1)
                pool.tensor_tensor(quart[:, :, :, :], half[:, 0:E // 4], half[:, E // 4:E // 2], ALU.add).then_inc(s_tree, 1)
                pool.wait_ge(s_tree, b * (2 * (T // 2) + 1) + n + 1)
                pool.tensor_tensor(ysum[:, 2 * g:2 * g + 2, :], quart[:, 0], quart[:, 1], ALU.add).then_inc(s_tail, 1)
                pool.wait_ge(s_tail, n + 1)

        @block.tensor
        def _(pe):
            def take(part, name, i):
                k, _, before = place(part, name, i)
                if before:
                    pe.wait_ge(*release(*before))
                return ring[:, k]

            def flat(buf):
                return buf.rearrange("p a n -> p (a n)")

            def project_qk(part, i, b, which, name):
                buf = take(part, name, i)
                if name == "q+":
                    pe.wait_ge(s_xs, b + 2)
                for h in range(2):
                    if name == "q":
                        pe.wait_ge(s_xs, h + 1)
                    rows = xst[:, chunk(h)]
                    pe.matmul(buf[0:ROW, h, :], w1[:, which].rearrange("p r m -> p (r m)"), rows, start=True, stop=False)
                    mm = pe.matmul(buf[0:ROW, h, :], w2[:, which].rearrange("p r m -> p (r m)"), rows, start=False, stop=True)
                    if name in ("q", "k") and h == 0:
                        mm.then_inc(s_qk0, 1)
                mm.then_inc(s_fill, 1)

            def project_v(part, i, name):
                buf = take(part, name, i)
                for tile in range(T):
                    toks = xst[:, col(tile):col(tile) + P]
                    o = (tile % 4) * (M + C)
                    pe.matmul(buf[:, tile // 4, o:o + M + C], toks, vx1[:, :], start=True, stop=False)
                    mm = pe.matmul(buf[:, tile // 4, o:o + M + C], toks, vx2[:, :], start=False, stop=True)
                mm.then_inc(s_fill, 1)

            def max_scores(part, i, b, tile):
                buf = take(part, f"mx{tile}", i)
                if tile == 0:
                    pe.wait_ge(s_qks, 2 * (b + 2))
                for h in range(2):
                    mm = pe.matmul(buf[:, h, :], kst[0:ROW, col(tile):col(tile) + P], qst[0:ROW, chunk(h)],
                                   start=True, stop=True)
                mm.then_inc(s_fill, 1)

            def max_row(part, i, b):
                buf = take(part, "mrow", i)
                pe.wait_ge(s_nm, 2 * (b + 1))
                for tile in range(T):
                    c = col(tile)
                    mm = pe.matmul(flat(buf)[0:ROW + 2, c:c + P], nmax[:, tile, :], ident_r[:, :], start=True, stop=True)
                mm.then_inc(s_fill, 1)

            def scores1(part, i, b, j):
                buf = take(part, f"st{j}", i)
                if j == 0:
                    pe.wait_ge(s_mrow, 2 * (b + 1))
                for h in range(2):
                    mm = pe.matmul(buf[:, h, :], qst[0:ROW + 2, col(j):col(j) + P], kst[0:ROW + 2, chunk(h)],
                                   start=True, stop=True)
                mm.then_inc(s_fill, 1)

            def weigh(acc, stationary, prob, j, s_p, s_sum, b):
                pe.wait_ge(s_p, T * b + j + 1)
                for h in range(2):
                    mm = pe.matmul(acc[h * C:(h + 1) * C, :], stationary[:, j, :], prob[:, j % 2, chunk(h)],
                                   start=(j == 0), stop=(j == T - 1))
                if j == T - 1:
                    mm.then_inc(s_sum, 1)

            def project_out(part, i, b):
                buf = take(part, "po", i)
                pe.wait_ge(s_agg, b + 1)
                for t in range(4):
                    o = (t % 2) * 2 * (C + 1)
                    mm = pe.matmul(buf[:, t // 2, o:o + 2 * (C + 1)], agg[:, t * P:(t + 1) * P],
                                   wo_blk[:, :, :].rearrange("p h c -> p (h c)"), start=True, stop=True)
                mm.then_inc(s_fill, 1)

            def u_transposed(b):
                pe.wait_ge(s_gbs, b + 1)
                pe.wait_ge(s_uh, b + 1)
                pe.wait_ge(s_u, b + 1)
                for which, bank in ((1, acc2), (0, acc1)):
                    for tile in range(T):
                        c = col(tile)
                        mm = pe.transpose(bank[:, :].bitcast(F16)[:, c:c + P],
                                          uhl[:, tile, which:which + 2, :].rearrange("p a c -> p (a c)"), ident_h[:, :])
                    mm.then_inc(s_uT, 1)

            def scores2(part, i, b, j):
                buf = take(part, f"s{j}", i)
                if j == 0:
                    pe.wait_ge(s_z, 2 * (b + 1))
                z = zst[:, col(j):col(j) + P]
                for h in range(2):
                    pe.matmul(buf[:, h, :], z, zst[:, chunk(h)], start=True, stop=False)
                    mm = pe.matmul(buf[:, h, :], z, zsw[:, chunk(h)], start=False, stop=True)
                mm.then_inc(s_fill, 1)

            y_flat = y[:, :, :].rearrange("p t c -> p (t c)")

            def back_transposed(part, i, name, src, s_src, value):
                buf = take(part, name, i)
                pe.wait_ge(s_src, value)
                for t in range(4):
                    mm = pe.transpose(buf[:, 0, t * P:(t + 1) * P], src[:, t * P:(t + 1) * P], ident[:, :])
                mm.then_inc(s_fill, 1)

            def att2_transposed(b):
                pe.wait_ge(s_att2, b + 1)
                for t in range(4):
                    mm = pe.transpose(acc2[:, t * P:(t + 1) * P], att2[:, t * P:(t + 1) * P], ident[:, :])
                mm.then_inc(s_o, 1)

            def w_transposed(part, i, b):
                buf = take(part, "wT", i)
                for h in range(2):
                    pe.wait_ge(s_w, 2 * b + h + 1)
                    for tile in range(h, T, 2):
                        c = col(tile)
                        mm = pe.transpose(flat(buf)[:, c:c + P], wdup[:, tile].rearrange("p a c -> p (a c)"), ident[:, :])
                    mm.then_inc(s_fill if h else s_wT, 1)

            def route(part, i, b):
                buf = take(part, "rt", i)
                pe.wait_ge(s_ws, 2 * (b + 1))
                for tile in range(T):
                    toks = wst[:, col(tile):col(tile) + P]
                    mm = pe.matmul(buf[:, 0, tile * 2 * E:(tile + 1) * 2 * E], toks, r12[:, :, :].rearrange("p a e -> p (a e)"),
                                   start=True, stop=True)
                mm.then_inc(s_fill, 1)

            def experts(part, i, b, g):
                buf = take(part, f"e{g}", i)
                for h in range(2):
                    toks = wst[:, col(2 * g + h):col(2 * g + h) + P]
                    pe.matmul(buf[:, h, :], toks, e1[:, :], start=True, stop=False)
                    mm = pe.matmul(buf[:, h, :], toks, e2[:, :], start=False, stop=True)
                mm.then_inc(s_fill, 1)

            def gates_transposed(b):
                pe.wait_ge(s_oT, b + 1)
                pe.wait_ge(s_gate, b + 1)
                pe.transpose(acc2[:, 0:P], gate[:, :, :].rearrange("p t e -> p (t e)"), ident[:, :]).then_inc(s_gT, 1)

            def expert_bias(b):
                pe.wait_ge(s_gt, b + 1)
                pe.matmul(acc2[:, :], gate_t[:, :], eb_blk[:, :, :].rearrange("p t c -> p (t c)"),
                          start=True, stop=True).then_inc(s_gb, 1)

            def keep_clock(n):
                for _ in range(n):
                    pe.matmul(acc1[:, :], filler[:, 0:P], filler[:, :], start=True, stop=True)

            pe.wait_ge(s_filler, 1)
            keep_clock(9)
            buf = take("first", "w3", 0)
            pe.wait_ge(s_const, 2)
            pe.wait_ge(s_w3, 3 * 16)
            pe.transpose(buf[:, 0, 0:ROW], w3[:, :, :].rearrange("p a c -> p (a c)"), ident[0:ROW, 0:ROW]).then_inc(s_fill, 1)
            keep_clock(2)
            pe.wait_ge(s_wts, 3)
            project_qk("first", 0, 0, 0, "q")
            project_qk("first", 0, 0, 1, "k")
            project_v("first", 0, "vx")
            for tile in range(T):
                max_scores("first", 0, 0, tile)
                if tile >= RING - 1:
                    keep_clock(2)
            pe.wait_ge(s_wol, 2 * 16)
            pe.transpose(acc2[:, 0:C], wo4[:, :, :].rearrange("p a m -> p (a m)"), ident[0:C, 0:C]).then_inc(s_woT, 1)
            keep_clock(7)
            max_row("first", 0, 0)
            keep_clock(3)
            for j in range(T):
                scores1("first", 0, 0, j)
                if j:
                    weigh(acc1, val, prob1, j - 1, s_p1, s_av1, 0)
            project_qk("first", 0, 1, 0, "q+")
            weigh(acc1, val, prob1, T - 1, s_p1, s_av1, 0)
            project_qk("first", 0, 1, 1, "k+")
            pe.wait_ge(s_wblk, 2)
            project_out("first", 0, 0)
            project_v("first", 0, "vx+")
            pe.wait_ge(s_es, 3)
            keep_clock(26)
            u_transposed(0)
            for k in range(RING):
                pe.wait_ge(*release(last_use(FIRST, k), "first", 0))

            with pe.Fori(0, B - 1) as i:
                for j in range(T):
                    if j == 7:
                        max_row("body", i, i + 1)
                    scores2("body", i, i, j)
                    for tile in MX_AT[j]:
                        max_scores("body", i, i + 1, tile)
                    if j:
                        weigh(acc2, u, prob2, j - 1, s_p2, s_av2, i)
                    if j == 5:
                        back_transposed("body", i, "yT-", y_flat, s_y, i + 1)
                scores1("body", i, i + 1, 0)
                weigh(acc2, u, prob2, T - 1, s_p2, s_av2, i)
                for j in range(1, T):
                    scores1("body", i, i + 1, j)
                    if j == 1:
                        att2_transposed(i)
                    if j == 7:
                        route("body", i, i)
                    weigh(acc1, val, prob1, j - 1, s_p1, s_av1, i + 1)
                    if j == 5:
                        w_transposed("body", i, i)
                project_qk("body", i, i + 2, 0, "q+")
                weigh(acc1, val, prob1, T - 1, s_p1, s_av1, i + 1)
                project_qk("body", i, i + 2, 1, "k+")
                project_out("body", i, i + 1)
                gates_transposed(i)
                experts("body", i, i, 0)
                experts("body", i, i, 1)
                expert_bias(i)
                project_v("body", i, "vx+")
                keep_clock(4)
                experts("body", i, i, 3)
                keep_clock(4)
                u_transposed(i + 1)
                experts("body", i, i, 2)

            b = B - 1
            for j in range(T):
                scores2("last", b, b, j)
                if j:
                    weigh(acc2, u, prob2, j - 1, s_p2, s_av2, b)
            weigh(acc2, u, prob2, T - 1, s_p2, s_av2, b)
            att2_transposed(b)
            back_transposed("last", b, "yT-", y_flat, s_y, b + 1)
            keep_clock(26)
            w_transposed("last", b, b)
            keep_clock(4)
            route("last", b, b)
            experts("last", b, b, 0)
            experts("last", b, b, 1)
            experts("last", b, b, 2)
            keep_clock(8)
            gates_transposed(b)
            keep_clock(5)
            experts("last", b, b, 3)
            pe.wait_ge(s_tk2, B)
            pe.wait_ge(s_gt, B)
            for t in SUM_ORDER:
                part_sum = (acc1, acc2)[t // 2][:, t % 2 * P:(t % 2 + 1) * P]
                pe.matmul(part_sum, tok2[:, 2 * t:2 * t + 2, :].rearrange("p h c -> p (h c)"), ident[:, :],
                          start=True, stop=False)
                pe.matmul(part_sum, eb_blk[:, 2 * t:2 * t + 2, :].rearrange("p h c -> p (h c)"), gate_t[:, :],
                          start=False, stop=False)
                if t in ON_POOL or t == ON_VECTOR:
                    if t in ON_POOL:
                        pe.wait_ge(s_tail, ON_POOL.index(t) + 1)
                    else:
                        pe.wait_ge(s_tail_v, 1)
                    mm = pe.matmul(part_sum, ysum[:, 2 * t:2 * t + 2, :].rearrange("p h c -> p (h c)"), ident[:, :],
                                   start=False, stop=True)
                else:
                    pe.wait_ge(s_prod, (T // 2) * B + t + 1)
                    for e in range(E):
                        mm = pe.matmul(part_sum, prod[:, t, e].rearrange("p h c -> p (h c)"), ident[:, :],
                                       start=False, stop=(e == E - 1))
                mm.then_inc(s_yT, 1)

        @block.scalar
        def _(act):
            def filled(part, name, i):
                k, n, _ = place(part, name, i)
                act.wait_ge(s_fill, n + 1)
                return ring[:, k]

            def flat(buf):
                return buf.rearrange("p a n -> p (a n)")

            def round_x(slot):
                act.activation(xst[:, :], slot, ACT.Copy).then_inc(s_xr, 1)

            def round_qk(part, i, name, dst):
                act.activation(dst[0:ROW, :], flat(filled(part, name, i))[0:ROW, :], ACT.Copy)

            def keep_whole(part, i, name, rows, s):
                buf = filled(part, name, i)
                act.activation(qk_f[rows, :], flat(buf)[rows, :], ACT.Copy).then_inc(s, 1)

            def values(part, i, b, name):
                buf = filled(part, name, i)
                b4 = buf[:, :, 0:4 * (M + C)].rearrange("p a (t c) -> p a t c", c=M + C)
                act.activation(val[:, :, 0:M].rearrange("p (a t) c -> p a t c", a=2), b4[:, :, :, 0:M],
                               ACT.Copy).then_inc(s_vx, 1)
                act.wait_ge(s_tk1, b)
                act.activation(xt[:, :, :].rearrange("p (a t) c -> p a t c", a=2), b4[:, :, :, M:M + C],
                               ACT.Copy).then_inc(s_vx, 1)

            def max_row(part, i):
                buf = filled(part, "mrow", i)
                act.activation(kst[ROW:ROW + 2, 0:CHUNK], buf[ROW:ROW + 2, 0, :], ACT.Copy).then_inc(s_mrow, 1)

            def exp1(part, i, j):
                act.activation(prob1[:, j % 2, :], flat(filled(part, f"st{j}", i)), ACT.Exp).then_inc(s_p1, 1)

            def exp2(part, i, j):
                act.activation(prob2[:, j % 2, :], flat(filled(part, f"s{j}", i)), ACT.Exp, bias=shift[:, :],
                               accum_out=rsum2[:, j:j + 1]).then_inc(s_p2, 1)

            def copy_sums(dst, src, s_sum, b, s_ready):
                act.wait_ge(s_sum, b + 1)
                act.activation(dst, src, ACT.Copy).then_inc(s_ready, 1)

            def copy_high(b):
                act.wait_ge(s_un, b + 1)
                act.activation(uhl[:, :, 2, :], u[:, :, :], ACT.Copy).then_inc(s_uh, 1)

            def stack_swapped(b):
                act.wait_ge(s_uT, 2 * b + 1)
                act.activation(zsw[:, :], acc2[:, :].bitcast(F16), ACT.Copy).then_inc(s_z, 1)

            def round_w(part, i, b):
                k, used, _ = place(part, "wT", i)
                for h in range(2):
                    if h:
                        act.wait_ge(s_fill, used + 1)
                    else:
                        act.wait_ge(s_wT, b + 1)
                    act.activation(wst[:, chunk(h)], ring[:, k, h, :], ACT.Copy).then_inc(s_wr, 1)

            def gap_exp(b):
                act.wait_ge(s_gap, b + 1)
                act.activation(gm[:, 3, :], gm[:, 2, :], ACT.Exp).then_inc(s_eg, 1)

            def copy_gates(b):
                act.wait_ge(s_gT, b + 1)
                act.activation(gate_t[:, :], acc2[0:T * E, 0:P], ACT.Copy).then_inc(s_gt, 1)

            def result(part, name, i, image):
                buf = filled(part, name, i)
                act.wait_ge(s_ob_free, image + 1)
                act.activation(ob[:, :], buf[:, 0, :], ACT.Copy).then_inc(s_ob, 1)

            act.wait_ge(s_x[0], 32)
            for h in range(2):
                act.activation(xst[:, chunk(h)], xin[:, 0, chunk(h)], ACT.Copy).then_inc(s_xr, 1)
            buf = filled("first", "w3", 0)
            for r in range(3):
                act.activation(w1[:, :, r, :], buf[:, 0, 0:2 * M].rearrange("p (a m) -> p a m", a=2), ACT.Copy).then_inc(s_wr1, 1)
            act.activation(vx1[:, 0:M], buf[:, 0, 2 * M:3 * M], ACT.Copy).then_inc(s_wr1, 1)
            for name, dst, s_rounded in (("q", qst, s_qr), ("k", kst, s_kr)):
                k, used, _ = place("first", name, 0)
                for h in range(2):
                    if h == 0:
                        act.wait_ge(s_qk0, 1 if name == "q" else 2)
                    else:
                        act.wait_ge(s_fill, used + 1)
                    act.activation(dst[0:ROW, chunk(h)], ring[0:ROW, k, h, :], ACT.Copy).then_inc(s_rounded, 1)
            values("first", 0, 0, "vx")
            act.wait_ge(s_x[1], 32)
            round_x(xin[:, 1, :])
            act.wait_ge(s_ew, (5 + T) * 16)
            act.activation(e1[:, :], e_in[:, :, :].rearrange("p e c -> p (e c)"), ACT.Copy).then_inc(s_er, 1)
            act.activation(r12[:, 0, :], r_in[:, :], ACT.Copy).then_inc(s_er, 1)
            max_row("first", 0)
            for j in range(T):
                exp1("first", 0, j)
            round_qk("first", 0, "q+", qst)
            copy_sums(agg[:, :], acc1[:, :], s_av1, 0, s_agg)
            keep_whole("first", 0, "q+", slice(M, 2 * M), s_qf)
            round_qk("first", 0, "k+", kst)
            keep_whole("first", 0, "k+", slice(2 * M, 3 * M), s_kf)
            values("first", 0, 1, "vx+")
            copy_high(0)
            stack_swapped(0)
            act.wait_ge(s_shift, 1)
            for b in range(2, B):
                act.wait_ge(s_x[b], 32)

            with act.Fori(0, B - 1) as i:
                for j in range(T - 1):
                    exp2("body", i, j)
                    if j == 4:
                        round_x(xin[:, bass.ds(i + 2, 1), :].rearrange("p a n -> p (a n)"))
                result("body", "yT-", i, i)
                max_row("body", i)
                exp2("body", i, T - 1)
                exp1("body", i, 0)
                copy_sums(att2[:, :], acc2[:, :], s_av2, i, s_att2)
                for j in range(1, T):
                    exp1("body", i, j)
                    if j == 5:
                        round_w("body", i, i)
                gap_exp(i)
                round_qk("body", i, "q+", qst)
                copy_sums(agg[:, :], acc1[:, :], s_av1, i + 1, s_agg)
                keep_whole("body", i, "q+", slice(M, 2 * M), s_qf)
                round_qk("body", i, "k+", kst)
                copy_gates(i)
                keep_whole("body", i, "k+", slice(2 * M, 3 * M), s_kf)
                values("body", i, i + 2, "vx+")
                copy_sums(ybias[:, :, :].rearrange("p t c -> p (t c)"), acc2[:, :], s_gb, i, s_gbs)
                copy_high(i + 1)
                stack_swapped(i + 1)

            b = B - 1
            for j in range(T):
                exp2("last", b, j)
            copy_sums(att2[:, :], acc2[:, :], s_av2, b, s_att2)
            result("last", "yT-", b, b)
            round_w("last", b, b)
            gap_exp(b)
            copy_gates(b)
            act.wait_ge(s_ob_free, B + 1)
            for half_sum in range(2):
                act.wait_ge(s_yT, 2 * (half_sum + 1))
                cols = slice(half_sum * CHUNK // 2, (half_sum + 1) * CHUNK // 2)
                act.activation(ob[:, cols], (acc1, acc2)[half_sum][:, 0:CHUNK // 2], ACT.Copy).then_inc(s_ob, 1)

        @block.vector
        def _(dve):
            def filled(part, name, i):
                k, n, _ = place(part, name, i)
                dve.wait_ge(s_fill, n + 1)
                return ring[:, k]

            def flat(buf):
                return buf.rearrange("p a n -> p (a n)")

            def wide(a, n):
                return a.unsqueeze(2).to_broadcast([P, T, n])

            def row_max(part, i, tile):
                dve.tensor_reduce(rowmax[:, tile:tile + 1], flat(filled(part, f"mx{tile}", i)), AX.X, ALU.max).then_inc(s_mx, 1)

            def negate_max(b):
                dve.wait_ge(s_mx, T * (b + 1))
                hi = nmax[:, :, ROW:ROW + 1]
                rm = rowmax[:, :].unsqueeze(2)
                dve.tensor_scalar(hi, rm, -1.0, None, ALU.mult).then_inc(s_nm, 1)
                dve.wait_ge(s_nm, 2 * b + 1)
                dve.scalar_tensor_tensor(out=nmax[:, :, ROW + 1:ROW + 2], in0=rm, scalar=-1.0, in1=hi.bitcast(F32),
                                         op0=ALU.mult, op1=ALU.subtract).then_inc(s_nm, 1)

            def max_row(part, i):
                buf = filled(part, "mrow", i)
                dve.tensor_copy(kst[ROW:ROW + 2, CHUNK:N], buf[ROW:ROW + 2, 1, :]).then_inc(s_mrow, 1)

            def tokens1(part, i, b):
                buf = filled(part, "po", i)
                po = buf[:, :, 0:4 * (C + 1)].rearrange("p a (t c) -> p a t c", c=C + 1)
                r4 = rinv1[:, :].rearrange("p (a t) -> p a t", a=2).unsqueeze(3)
                dve.reciprocal(r4, po[:, :, :, C:C + 1]).then_inc(s_t1, 1)
                dve.wait_ge(s_t1, b + 1)
                dve.tensor_tensor(tdiv[:, :, :].rearrange("p (a t) c -> p a t c", a=2), po[:, :, :, 0:C],
                                  r4.to_broadcast([P, 2, 4, C]), ALU.mult).then_inc(s_po, 1)
                dve.wait_ge(s_po, b + 1)
                dve.wait_ge(s_vx, 2 * b + 2)
                dve.tensor_tensor(tok1[:, :, :], tdiv[:, :, :], xt[:, :, :], ALU.add).then_inc(s_tk1, 1)

            def norm_stats(tok, s_tok, stats, sm, cen, s_ln, s_ve, s_cen, b):
                dve.wait_ge(s_tok, b + 1)
                ln = Steps(dve, s_ln, 3, b)
                for tile in range(T):
                    last = dve.bn_stats(stats[:, tile, :], tok[:, tile, :])
                ln.then(last)
                mean_e, var_e, mean_o, var_o = (stats[:, :, k] for k in (1, 2, 4, 5))
                dve.tensor_tensor(sm[:, 0, :], mean_e, mean_o, ALU.subtract)
                dve.scalar_tensor_tensor(out=sm[:, 4, :], in0=var_e, scalar=C * EPS, in1=var_o, op0=ALU.add, op1=ALU.add)
                ln.then(dve.tensor_tensor(sm[:, 1, :], mean_e, mean_o, ALU.add))
                dve.scalar_tensor_tensor(out=sm[:, 5, :], in0=sm[:, 0, :], scalar=C / 4.0, in1=sm[:, 0, :],
                                         op0=ALU.mult, op1=ALU.mult)
                ln.then(dve.tensor_scalar(sm[:, 6, :], sm[:, 1, :], -ROOT_C / 2, None, ALU.mult))
                ln.end()
                dve.tensor_tensor(sm[:, 2, :], sm[:, 4, :], sm[:, 5, :], ALU.add).then_inc(s_ve, 1)
                dve.scalar_tensor_tensor(out=cen[:, :, :], in0=tok[:, :, :], scalar=ROOT_C, in1=wide(sm[:, 6, :], C),
                                         op0=ALU.mult, op1=ALU.add).then_inc(s_cen, 1)

            def normalize1(b):
                dve.wait_ge(s_cen1, b + 1)
                dve.wait_ge(s_rs1, b + 1)
                dve.tensor_tensor(u[:, :, :], cen1[:, :, :], wide(sm1[:, 3, :], C), ALU.mult).then_inc(s_un, 1)
                dve.wait_ge(s_un, b + 1)
                dve.tensor_copy(uhl[:, :, 0, :], u[:, :, :]).then_inc(s_uh1, 1)
                dve.wait_ge(s_uh1, b + 1)
                dve.tensor_tensor(uhl[:, :, 1, :], u[:, :, :], uhl[:, :, 0, :], ALU.subtract).then_inc(s_u, 1)

            def stack_u(b):
                dve.wait_ge(s_uT, 2 * b + 2)
                dve.tensor_copy(zst[:, :], acc1[:, :].bitcast(F16)).then_inc(s_z, 1)

            def tokens2(b):
                dve.wait_ge(s_p2, T * (b + 1))
                dve.reciprocal(rinv2[:, :], rsum2[:, :]).then_inc(s_t2, 1)
                dve.wait_ge(s_t2, b + 1)
                dve.wait_ge(s_o, b + 1)
                dve.tensor_tensor(odiv[:, :, :], acc2[:, :].rearrange("p (t c) -> p t c", c=C), wide(rinv2[:, :], C),
                                  ALU.mult).then_inc(s_oT, 1)
                dve.wait_ge(s_oT, b + 1)
                dve.wait_ge(s_y, b + 1)
                dve.tensor_tensor(tok2[:, :, :], odiv[:, :, :], tok1[:, :, :], ALU.add).then_inc(s_tk2, 1)

            def normalize2(b):
                dve.wait_ge(s_cen2, b + 1)
                dve.wait_ge(s_rs2, b + 1)
                for h in range(2):
                    tiles = slice(h, T, 2)
                    shape = [P, T // 2, 2, C]
                    dve.tensor_tensor(wdup[:, tiles, :, :], cen2[:, tiles, :].unsqueeze(2).to_broadcast(shape),
                                      sm2[:, 3, tiles].unsqueeze(2).unsqueeze(3).to_broadcast(shape), ALU.mult).then_inc(s_w, 1)

            def split_w(part, i, b):
                k, _, _ = place(part, "wT", i)
                for h in range(2):
                    dve.wait_ge(s_wr, 2 * b + h + 1)
                    lo = wst[C:P, chunk(h)]
                    dve.tensor_tensor(lo, ring[C:P, k, h, :], lo.bitcast(F32), ALU.subtract).then_inc(s_ws, 1)

            def top2(part, i, b):
                buf = filled(part, "rt", i)
                parts = buf[:, 0, 0:2 * T * E].rearrange("p (t a e) -> p t a e", a=2, e=E)
                dve.tensor_tensor(lg_1[:, :, :], parts[:, :, 0, :],
                                  rb_all[:, :].unsqueeze(1).to_broadcast([P, T, E]), ALU.add).then_inc(s_lg1, 1)
                dve.wait_ge(s_lg1, b + 1)
                dve.tensor_tensor(lg[:, :, :], parts[:, :, 1, :], lg_1[:, :, :], ALU.add).then_inc(s_lg, 1)
                dve.wait_ge(s_lg, b + 1)
                top = Steps(dve, s_top, 9, b)
                dve.tensor_copy(landing[:, :], lg[:, 0, 0:1])
                for tile in range(T):
                    last = dve.max(top8[:, tile, :], lg[:, tile, :])
                top.then(last)
                dve.tensor_tensor(gm[:, 2, :], top8[:, :, 1], top8[:, :, 0], ALU.subtract).then_inc(s_gap, 1)
                both = lg[:, :, :].unsqueeze(1).to_broadcast([P, 2, T, E])
                top.then(dve.tensor_tensor(cand[:, :, :, :], both, top8[:, :, 0:2].rearrange("p t n -> p n t").unsqueeze(3)
                                           .to_broadcast([P, 2, T, E]), ALU.is_equal))
                top.then(dve.tensor_tensor(cand[:, :, :, :], cand[:, :, :, :],
                                           ramp[:, :, :].unsqueeze(1).to_broadcast([P, 2, T, E]), ALU.mult))
                top.then(dve.tensor_reduce(gm[:, 0, :], cand[:, 0, :, :], AX.X, ALU.max))
                top.then(dve.tensor_tensor(pick1[:, :, :], cand[:, 0, :, :], wide(gm[:, 0, :], E), ALU.is_equal))
                dve.scalar_tensor_tensor(out=cand2[:, :, :], in0=pick1[:, :, :], scalar=-2.0 * E, in1=cand[:, 1, :, :],
                                         op0=ALU.mult, op1=ALU.add)
                dve.wait_ge(s_eg, b + 1)
                top.then(dve.tensor_scalar(gm[:, 4, :], gm[:, 3, :], 1.0, None, ALU.add))
                dve.tensor_reduce(gm[:, 1, :], cand2[:, :, :], AX.X, ALU.max)
                top.then(dve.reciprocal(gm[:, 5, :], gm[:, 4, :]))
                dve.tensor_tensor(pick2[:, :, :], cand2[:, :, :], wide(gm[:, 1, :], E), ALU.is_equal)
                top.then(dve.tensor_tensor(gm[:, 6, :], gm[:, 3, :], gm[:, 5, :], ALU.mult))
                dve.tensor_tensor(pick2[:, :, :], pick2[:, :, :], wide(gm[:, 6, :], E), ALU.mult)
                top.then(dve.tensor_tensor(pick1[:, :, :], pick1[:, :, :], wide(gm[:, 5, :], E), ALU.mult))
                top.end()
                dve.tensor_tensor(gate[:, 0:T, :], pick1[:, :, :], pick2[:, :, :], ALU.add).then_inc(s_gate, 1)

            def weigh_experts(part, i, b, g):
                buf = filled(part, f"e{g}", i)
                if g == 0:
                    dve.wait_ge(s_gate, b + 1)
                dve.wait_ge(s_half, (T // 2) * b + g + 1)
                gates = gate[:, 2 * g:2 * g + 2, :].unsqueeze(3).to_broadcast([P, 2, E, C])
                dve.tensor_tensor(prod[:, g].rearrange("p e h c -> p h e c"), buf.rearrange("p h (e c) -> p h e c", c=C),
                                  gates, ALU.mult).then_inc(s_prod, 1)

            def split_x0(h):
                dve.wait_ge(s_xr, h + 1)
                lo = xst[C:P, chunk(h)]
                dve.tensor_tensor(lo, xin[C:P, 0, chunk(h)], lo.bitcast(F32), ALU.subtract).then_inc(s_xs, 1)

            dve.memset(filler[:, :], 1.0).then_inc(s_filler, 1)
            dve.wait_ge(s_const, 2)
            dve.tensor_copy(ident_r[:, :], ident[:, :])
            dve.tensor_tensor(vx1[:, M:M + C], ident[:, 0:C], ident[:, C:P], ALU.add).then_inc(s_wts, 1)
            dve.memset(qst[ROW:ROW + 2, :].bitcast(F32), 1.0)
            dve.memset(shift[:, :], -SHIFT).then_inc(s_shift, 1)
            split_x0(0)
            buf = filled("first", "w3", 0)
            dve.wait_ge(s_wr1, 4)
            dve.tensor_tensor(w2[:, :, :, :], buf[:, 0, 0:2 * M].rearrange("p (a m) -> p a m", a=2).unsqueeze(2)
                              .to_broadcast([P, 2, 3, M]), w1[:, :, :, :].bitcast(F32), ALU.subtract).then_inc(s_wts, 1)
            dve.memset(vx2[:, M:M + C].bitcast(F32), 0.0)
            dve.tensor_tensor(vx2[:, 0:M], buf[:, 0, 2 * M:3 * M], vx1[:, 0:M].bitcast(F32), ALU.subtract).then_inc(s_wts, 1)
            split_x0(1)
            for name, dst, rows, s_rounded in (("q", qst, slice(M, 2 * M), s_qr), ("k", kst, slice(2 * M, 3 * M), s_kr)):
                k, _, _ = place("first", name, 0)
                for h in range(2):
                    dve.wait_ge(s_rounded, h + 1)
                    lo = dst[rows, chunk(h)]
                    dve.tensor_tensor(lo, ring[rows, k, h, :], lo.bitcast(F32), ALU.subtract).then_inc(s_qks, 1)
            for tile in range(T):
                row_max("first", 0, tile)
            dve.wait_ge(s_const, 4)
            negate_max(0)
            max_row("first", 0)
            dve.wait_ge(s_woT, 1)
            for h in range(2):
                dve.memset(wo_blk[h * C + ONE:h * C + ONE + 1, h, C:C + 1], 1.0)
                dve.tensor_copy(wo_blk[h * C:(h + 1) * C, h, 0:C], acc2[h * C:(h + 1) * C, 0:C]).then_inc(s_wblk, 1)
            dve.tensor_copy(ident_h[:, :], ident[:, :])
            dve.wait_ge(s_er, 2)
            dve.tensor_tensor(e2[:, :], e_in[:, :, :].rearrange("p e c -> p (e c)"), e1[:, :].bitcast(F32),
                              ALU.subtract).then_inc(s_es, 1)
            dve.tensor_tensor(r12[:, 1, :], r_in[:, :], r12[:, 0, :].bitcast(F32), ALU.subtract).then_inc(s_es, 1)
            dve.wait_ge(s_const, 5)
            dve.tensor_tensor(eb_blk[:, :, :], eb_in[:, :].unsqueeze(1).to_broadcast([T * E, T, C]),
                              tile_mask[:, :].unsqueeze(2).to_broadcast([T * E, T, C]), ALU.mult).then_inc(s_es, 1)
            tokens1("first", 0, 0)
            norm_stats(tok1, s_tk1, stats1, sm1, cen1, s_ln1, s_ve1, s_cen1, 0)
            normalize1(0)
            stack_u(0)

            with dve.Fori(0, B - 1) as i:
                for tile in range(T):
                    row_max("body", i, tile)
                negate_max(i + 1)
                max_row("body", i)
                tokens2(i)
                norm_stats(tok2, s_tk2, stats2, sm2, cen2, s_ln2, s_ve2, s_cen2, i)
                normalize2(i)
                split_w("body", i, i)
                top2("body", i, i)
                tokens1("body", i, i + 1)
                norm_stats(tok1, s_tk1, stats1, sm1, cen1, s_ln1, s_ve1, s_cen1, i + 1)
                weigh_experts("body", i, i, 0)
                normalize1(i + 1)
                weigh_experts("body", i, i, 1)
                stack_u(i + 1)
                weigh_experts("body", i, i, 2)
                weigh_experts("body", i, i, 3)

            b = B - 1
            tokens2(b)
            norm_stats(tok2, s_tk2, stats2, sm2, cen2, s_ln2, s_ve2, s_cen2, b)
            normalize2(b)
            split_w("last", b, b)
            top2("last", b, b)
            for g in range(T // 2):
                weigh_experts("last", b, b, g)
            t = ON_VECTOR
            dve.wait_ge(s_prod, (T // 2) * B + t + 1)
            dve.tensor_reduce(ysum[:, 2 * t:2 * t + 2, :], prod[:, t].rearrange("p e h c -> p h c e"), AX.X,
                              ALU.add).then_inc(s_tail_v, 1)


_INS = ["x", "L0_conv_wq", "L0_conv_wk", "L0_conv_wv", "L0_conv_wo", "L1_ffn_router_w", "L1_ffn_router_b",
        "L1_ffn_expert_w", "L1_ffn_expert_b"]


def kernel(**inputs):
    import numpy as _np
    import concourse.bacc as _bacc
    from concourse import mybir as _mybir
    from concourse.bass_utils import run_bass_kernel_spmd as _run

    nc = _bacc.Bacc("TRN2", target_bir_lowering=False, num_devices=1)
    arrays, args = {}, []
    for name in _INS:
        a = _np.ascontiguousarray(inputs[name])
        arrays[f"in_{name}"] = a
        args.append(nc.dram_tensor(f"in_{name}", a.shape, _mybir.dt.from_np(a.dtype), kind="ExternalInput").ap())
    shape = inputs["x"].shape
    args.append(nc.dram_tensor("out_0", shape, _mybir.dt.float32, kind="ExternalOutput").ap())
    build(nc, *args)
    return _run(nc, [arrays], core_ids=[0]).results[0]["out_0"]
```
